# Optimizing a Trainium2 kernel written in Bass

```python
import numpy as np
import jax
import jax.numpy as jnp

def _softmax(x, axis=-1):
    return jax.nn.softmax(x, axis=axis)

def _gelu(x):
    return jax.nn.gelu(x, approximate=True)

def _silu(x):
    return jax.nn.silu(x)

def _sigmoid(x):
    return jax.nn.sigmoid(x)

def _layernorm(x, axis=-1, eps=1e-05):
    m = jnp.mean(x, axis=axis, keepdims=True)
    v = jnp.var(x, axis=axis, keepdims=True)
    return (x - m) / jnp.sqrt(v + eps)

def _scatter_add(tgt, idx, src, axis=0):
    return tgt.at[idx].add(src)

def _segment_sum(src, seg, n):
    return jax.ops.segment_sum(src, seg, n)
kernel_name = 'mk_dlrm_tower_d1_rec_r8_22454a'

def setup_inputs(seed: int=0):
    np.random.seed(seed)
    _w = jnp.asarray

    def _rec_inputs():
        import jax
        import jax.numpy as jnp
        _tk = jax.random.key(seed)
        dense_ctx = jax.random.normal(jax.random.fold_in(_tk, 190), (1024, 16), jnp.float32)
        ids = jnp.stack([jax.random.randint(jax.random.fold_in(_tk, 200 + f), (1024,), 0, v, jnp.int32) for f, v in enumerate([12500, 125000, 12500, 12500, 1000, 1250, 1250, 1250, 125000, 1250, 1250, 1250, 1000, 1000, 12500, 1000, 1000, 125000, 1000, 1000, 12500, 12500, 1250, 1250, 1000, 12500, 125000, 12500, 12500, 1000, 1000, 125000])], axis=1)
        tbl_0 = 0.05 * jax.random.normal(jax.random.fold_in(_tk, 500 + 0), (12500, 16), jnp.float32)
        tbl_1 = 0.05 * jax.random.normal(jax.random.fold_in(_tk, 500 + 1), (125000, 16), jnp.float32)
        tbl_2 = 0.05 * jax.random.normal(jax.random.fold_in(_tk, 500 + 2), (12500, 16), jnp.float32)
        tbl_3 = 0.05 * jax.random.normal(jax.random.fold_in(_tk, 500 + 3), (12500, 16), jnp.float32)
        tbl_4 = 0.05 * jax.random.normal(jax.random.fold_in(_tk, 500 + 4), (1000, 16), jnp.float32)
        tbl_5 = 0.05 * jax.random.normal(jax.random.fold_in(_tk, 500 + 5), (1250, 16), jnp.float32)
        tbl_6 = 0.05 * jax.random.normal(jax.random.fold_in(_tk, 500 + 6), (1250, 16), jnp.float32)
        tbl_7 = 0.05 * jax.random.normal(jax.random.fold_in(_tk, 500 + 7), (1250, 16), jnp.float32)
        tbl_8 = 0.05 * jax.random.normal(jax.random.fold_in(_tk, 500 + 8), (125000, 16), jnp.float32)
        tbl_9 = 0.05 * jax.random.normal(jax.random.fold_in(_tk, 500 + 9), (1250, 16), jnp.float32)
        tbl_10 = 0.05 * jax.random.normal(jax.random.fold_in(_tk, 500 + 10), (1250, 16), jnp.float32)
        tbl_11 = 0.05 * jax.random.normal(jax.random.fold_in(_tk, 500 + 11), (1250, 16), jnp.float32)
        tbl_12 = 0.05 * jax.random.normal(jax.random.fold_in(_tk, 500 + 12), (1000, 16), jnp.float32)
        tbl_13 = 0.05 * jax.random.normal(jax.random.fold_in(_tk, 500 + 13), (1000, 16), jnp.float32)
        tbl_14 = 0.05 * jax.random.normal(jax.random.fold_in(_tk, 500 + 14), (12500, 16), jnp.float32)
        tbl_15 = 0.05 * jax.random.normal(jax.random.fold_in(_tk, 500 + 15), (1000, 16), jnp.float32)
        tbl_16 = 0.05 * jax.random.normal(jax.random.fold_in(_tk, 500 + 16), (1000, 16), jnp.float32)
        tbl_17 = 0.05 * jax.random.normal(jax.random.fold_in(_tk, 500 + 17), (125000, 16), jnp.float32)
        tbl_18 = 0.05 * jax.random.normal(jax.random.fold_in(_tk, 500 + 18), (1000, 16), jnp.float32)
        tbl_19 = 0.05 * jax.random.normal(jax.random.fold_in(_tk, 500 + 19), (1000, 16), jnp.float32)
        tbl_20 = 0.05 * jax.random.normal(jax.random.fold_in(_tk, 500 + 20), (12500, 16), jnp.float32)
        tbl_21 = 0.05 * jax.random.normal(jax.random.fold_in(_tk, 500 + 21), (12500, 16), jnp.float32)
        tbl_22 = 0.05 * jax.random.normal(jax.random.fold_in(_tk, 500 + 22), (1250, 16), jnp.float32)
        tbl_23 = 0.05 * jax.random.normal(jax.random.fold_in(_tk, 500 + 23), (1250, 16), jnp.float32)
        tbl_24 = 0.05 * jax.random.normal(jax.random.fold_in(_tk, 500 + 24), (1000, 16), jnp.float32)
        tbl_25 = 0.05 * jax.random.normal(jax.random.fold_in(_tk, 500 + 25), (12500, 16), jnp.float32)
        tbl_26 = 0.05 * jax.random.normal(jax.random.fold_in(_tk, 500 + 26), (125000, 16), jnp.float32)
        tbl_27 = 0.05 * jax.random.normal(jax.random.fold_in(_tk, 500 + 27), (12500, 16), jnp.float32)
        tbl_28 = 0.05 * jax.random.normal(jax.random.fold_in(_tk, 500 + 28), (12500, 16), jnp.float32)
        tbl_29 = 0.05 * jax.random.normal(jax.random.fold_in(_tk, 500 + 29), (1000, 16), jnp.float32)
        tbl_30 = 0.05 * jax.random.normal(jax.random.fold_in(_tk, 500 + 30), (1000, 16), jnp.float32)
        tbl_31 = 0.05 * jax.random.normal(jax.random.fold_in(_tk, 500 + 31), (125000, 16), jnp.float32)
        _rk = jax.random.fold_in(_tk, 7)
        W_top1 = 0.0693375 * jax.random.normal(jax.random.fold_in(_tk, 801), (208, 512), jnp.float32)
        W_top2 = 0.0441942 * jax.random.normal(jax.random.fold_in(_tk, 802), (512, 256), jnp.float32)
        W_top3 = 0.0625 * jax.random.normal(jax.random.fold_in(_tk, 803), (256, 1), jnp.float32)
        b_top1 = jnp.zeros((512,), jnp.float32)
        b_top2 = jnp.zeros((256,), jnp.float32)
        return (dense_ctx, ids, tbl_0, tbl_1, tbl_2, tbl_3, tbl_4, tbl_5, tbl_6, tbl_7, tbl_8, tbl_9, tbl_10, tbl_11, tbl_12, tbl_13, tbl_14, tbl_15, tbl_16, tbl_17, tbl_18, tbl_19, tbl_20, tbl_21, tbl_22, tbl_23, tbl_24, tbl_25, tbl_26, tbl_27, tbl_28, tbl_29, tbl_30, tbl_31, W_top1, b_top1, W_top2, b_top2, W_top3)
    dense_ctx, ids, tbl_0, tbl_1, tbl_2, tbl_3, tbl_4, tbl_5, tbl_6, tbl_7, tbl_8, tbl_9, tbl_10, tbl_11, tbl_12, tbl_13, tbl_14, tbl_15, tbl_16, tbl_17, tbl_18, tbl_19, tbl_20, tbl_21, tbl_22, tbl_23, tbl_24, tbl_25, tbl_26, tbl_27, tbl_28, tbl_29, tbl_30, tbl_31, W_top1, b_top1, W_top2, b_top2, W_top3 = _rec_inputs()

    def _L0_rec_setup():
        import jax, jax.numpy as jnp
        import numpy as np
        B, M, D = (2048, 32, 16)
        LAYERS = [64, 64, 64]
        key = jax.random.key(seed)
        ks = jax.random.split(key, 4)
        inp = {'embeddings': jax.random.normal(ks[0], (B, M, D), dtype=jnp.float32)}
        hk_1 = M
        for i, hk in enumerate(LAYERS):
            scale = (2.0 / (M * hk_1 + hk)) ** 0.5
            inp[f'W{i}'] = jax.random.normal(ks[i + 1], (M, hk_1, hk), dtype=jnp.float32) * scale
            hk_1 = hk
        return inp
    _L0_rec_all = _L0_rec_setup()
    _L0_rec_in = {k: v for k, v in _L0_rec_all.items() if k in ('W0', 'W1', 'W2')}
    del _L0_rec_all
    return {'dense_ctx': dense_ctx, 'ids': ids, 'tbl_0': tbl_0, 'tbl_1': tbl_1, 'tbl_2': tbl_2, 'tbl_3': tbl_3, 'tbl_4': tbl_4, 'tbl_5': tbl_5, 'tbl_6': tbl_6, 'tbl_7': tbl_7, 'tbl_8': tbl_8, 'tbl_9': tbl_9, 'tbl_10': tbl_10, 'tbl_11': tbl_11, 'tbl_12': tbl_12, 'tbl_13': tbl_13, 'tbl_14': tbl_14, 'tbl_15': tbl_15, 'tbl_16': tbl_16, 'tbl_17': tbl_17, 'tbl_18': tbl_18, 'tbl_19': tbl_19, 'tbl_20': tbl_20, 'tbl_21': tbl_21, 'tbl_22': tbl_22, 'tbl_23': tbl_23, 'tbl_24': tbl_24, 'tbl_25': tbl_25, 'tbl_26': tbl_26, 'tbl_27': tbl_27, 'tbl_28': tbl_28, 'tbl_29': tbl_29, 'tbl_30': tbl_30, 'tbl_31': tbl_31, 'W_top1': W_top1, 'b_top1': b_top1, 'W_top2': W_top2, 'b_top2': b_top2, 'W_top3': W_top3, 'L0_rec_W0': _L0_rec_in['W0'], 'L0_rec_W1': _L0_rec_in['W1'], 'L0_rec_W2': _L0_rec_in['W2']}

def reference(dense_ctx, ids, tbl_0, tbl_1, tbl_2, tbl_3, tbl_4, tbl_5, tbl_6, tbl_7, tbl_8, tbl_9, tbl_10, tbl_11, tbl_12, tbl_13, tbl_14, tbl_15, tbl_16, tbl_17, tbl_18, tbl_19, tbl_20, tbl_21, tbl_22, tbl_23, tbl_24, tbl_25, tbl_26, tbl_27, tbl_28, tbl_29, tbl_30, tbl_31, W_top1, b_top1, W_top2, b_top2, W_top3, L0_rec_W0, L0_rec_W1, L0_rec_W2):
    import jax
    import jax.numpy as jnp

    def _L0_rec_ref(embeddings, W0, W1, W2):
        import jax, jax.numpy as jnp
        import numpy as np
        B, M, D = (2048, 32, 16)
        LAYERS = [64, 64, 64]
        x0 = embeddings
        xk = x0
        outs = []
        for W in (W0, W1, W2):
            xk = jax.nn.relu(jnp.einsum('bmd,bhd,mhk->bkd', x0, xk, W))
            outs.append(jnp.sum(xk, axis=2))
        return jnp.concatenate(outs, axis=1)
    e = jnp.stack([tbl_0[ids[:, 0]], tbl_1[ids[:, 1]], tbl_2[ids[:, 2]], tbl_3[ids[:, 3]], tbl_4[ids[:, 4]], tbl_5[ids[:, 5]], tbl_6[ids[:, 6]], tbl_7[ids[:, 7]], tbl_8[ids[:, 8]], tbl_9[ids[:, 9]], tbl_10[ids[:, 10]], tbl_11[ids[:, 11]], tbl_12[ids[:, 12]], tbl_13[ids[:, 13]], tbl_14[ids[:, 14]], tbl_15[ids[:, 15]], tbl_16[ids[:, 16]], tbl_17[ids[:, 17]], tbl_18[ids[:, 18]], tbl_19[ids[:, 19]], tbl_20[ids[:, 20]], tbl_21[ids[:, 21]], tbl_22[ids[:, 22]], tbl_23[ids[:, 23]], tbl_24[ids[:, 24]], tbl_25[ids[:, 25]], tbl_26[ids[:, 26]], tbl_27[ids[:, 27]], tbl_28[ids[:, 28]], tbl_29[ids[:, 29]], tbl_30[ids[:, 30]], tbl_31[ids[:, 31]]], axis=1)
    z = _L0_rec_ref(e, L0_rec_W0, L0_rec_W1, L0_rec_W2)
    z = z.reshape(z.shape[0], -1)
    h = jnp.concatenate([z, dense_ctx], axis=1)
    h = jnp.maximum(h @ W_top1 + b_top1, 0.0)
    h = jnp.maximum(h @ W_top2 + b_top2, 0.0)
    y = h @ W_top3
    return y

_drawn_inputs = setup_inputs


def setup_inputs(seed=0):
    import zlib

    import numpy as np

    out = dict(_drawn_inputs(seed))
    spreads = {'b_top1': (0.0, 2.0), 'b_top2': (0.0, 0.8)}
    factors = {'tbl_0': 8.0,
     'tbl_1': 8.0,
     'tbl_2': 8.0,
     'tbl_3': 8.0,
     'tbl_4': 8.0,
     'tbl_5': 8.0,
     'tbl_6': 8.0,
     'tbl_7': 8.0,
     'tbl_8': 8.0,
     'tbl_9': 8.0,
     'tbl_10': 8.0,
     'tbl_11': 8.0,
     'tbl_12': 8.0,
     'tbl_13': 8.0,
     'tbl_14': 8.0,
     'tbl_15': 8.0,
     'tbl_16': 8.0,
     'tbl_17': 8.0,
     'tbl_18': 8.0,
     'tbl_19': 8.0,
     'tbl_20': 8.0,
     'tbl_21': 8.0,
     'tbl_22': 8.0,
     'tbl_23': 8.0,
     'tbl_24': 8.0,
     'tbl_25': 8.0,
     'tbl_26': 8.0,
     'tbl_27': 8.0,
     'tbl_28': 8.0,
     'tbl_29': 8.0,
     'tbl_30': 8.0,
     'tbl_31': 8.0,
     'L0_rec_W0': 3.465,
     'L0_rec_W1': 8.0,
     'L0_rec_W2': 8.0,
     'dense_ctx': 7.3}
    for name, (base, spread) in spreads.items():
        noise = np.random.default_rng([zlib.crc32(name.encode()), seed]).standard_normal(out[name].shape)
        drawn = base * np.exp(spread * noise) if base else spread * noise
        out[name] = jnp.asarray(drawn.astype(out[name].dtype))
    for name, factor in factors.items():
        out[name] = (out[name] * factor).astype(out[name].dtype)
    return out
```

```python
from contextlib import ExitStack

import concourse.bass as bass
from concourse import mybir

F32 = mybir.dt.float32
I32 = mybir.dt.int32
ALU = mybir.AluOpType
ACT = mybir.ActivationFunctionType
AX_X = mybir.AxisListType.X

P = 128
BATCH = 1024
FIELDS = 32
DIM = 16
HK = 64
LAYERS = 3
TILES = BATCH // P
PAIRS = 2 * TILES
D_CHUNK = 4
CHUNK = D_CHUNK * P
WIDE = 2 * CHUNK
ROWS = FIELDS * DIM
STEPS = FIELDS // 2

Q = P // FIELDS
SHIFT_TILES = 4
L0_UNITS = 2 * SHIFT_TILES
WRAP = P + Q * SHIFT_TILES

POOL_STEPS = (3, 7, 11, 15)
DVE_STEPS = tuple(t for t in range(STEPS) if t not in POOL_STEPS)
N_DVE, N_POOL = len(DVE_STEPS), len(POOL_STEPS)
DVE_RING, POOL_RING, L0_RING = 4, 2, 4
Z_STEP = 6

BLOCK = 4
BLOCKS = STEPS // BLOCK

H1, H2 = 512, 256
HALF = 512


def before(steps, block):
    return sum(t < BLOCK * (block + 1) for t in steps)


def cin_tower(nc, dense_ctx, ids, tables, w_top1, b_top1, w_top2, b_top2, w_top3,
              w0_ab, w0_ba, w0_diag, w1, w2, ident, out):
    with ExitStack() as ctx:
        def sb(name, shape, dt=F32):
            return ctx.enter_context(nc.sbuf_tensor(name, shape, dt))

        def psum(name, shape):
            return ctx.enter_context(nc.psum_tensor(name, shape, F32))

        def sem(name):
            return ctx.enter_context(nc.semaphore(name))

        x0_rows = nc.dram_tensor("x0_rows", (2, FIELDS, WIDE), F32, kind="Internal").ap()

        x0_wide = sb("x0_wide", [P, 6, BLOCK * WIDE])
        dve_ring = sb("dve_ring", [P, DVE_RING, WIDE])
        pool_ring = sb("pool_ring", [P, POOL_RING, WIDE])
        l0_ring = sb("l0_ring", [P, L0_RING, CHUNK])
        gathered = sb("gathered", [P, ROWS])
        repeated = sb("repeated", [P, WRAP * DIM])
        rotated = sb("rotated", [P, P * DIM])
        x0_rot = sb("x0_rot", [P, WIDE])
        squares = sb("squares", [FIELDS, WIDE])
        x_sb = [sb(f"x_sb{l}", [P, WIDE]) for l in range(2)]
        layer_out = sb("layer_out", [P, LAYERS, 2, CHUNK])
        z = sb("z", [P, LAYERS, BATCH])
        w0_sb = sb("w0_sb", [P, SHIFT_TILES, HK])
        w0b_sb = sb("w0b_sb", [P, SHIFT_TILES, HK])
        w0d_sb = sb("w0d_sb", [FIELDS, HK])
        w_sb = [sb(f"w_sb{l}", [P, STEPS, HK]) for l in (1, 2)]
        ident_sb = sb("ident_sb", [P, P])
        idx = sb("idx", [P, FIELDS], I32)

        acc = [psum(f"acc{i}", [P, CHUNK]) for i in range(2)]
        x_ps = [psum(f"x_ps{l}", [P, WIDE]) for l in range(2)]
        turned = psum("turned", [P, 2, CHUNK])

        free0 = x0_wide[:, 0:2, :].rearrange("p a n -> p (a n)")
        free1 = x0_wide[:, 2:4, :].rearrange("p a n -> p (a n)")
        taken = [0]

        def mlp(n, rows=P):
            taken[0] += n
            return free0[0:rows, taken[0] - n:taken[0]]

        wt1 = mlp(LAYERS * H1).rearrange("p (l j) -> p l j", l=LAYERS)
        wt1d = mlp(H1, DIM)
        wt2 = mlp(H1 // P * H2).rearrange("p (c j) -> p c j", j=H2)
        wt3 = mlp(H2 // P)
        b1 = mlp(H1 // P)
        b2 = mlp(H2 // P)
        dense = mlp(TILES * DIM).rearrange("p (t f) -> p t f", f=DIM)
        dense_t = mlp(BATCH, DIM)
        y_sb = mlp(BATCH, 1)
        h1 = free1[:, 0:H1 // P * BATCH].rearrange("p (c n) -> p c n", n=BATCH)
        h2 = free1[:, H1 // P * BATCH:(H1 + H2) // P * BATCH].rearrange("p (c n) -> p c n", n=BATCH)

        weights = sem("weights")
        weights_b = sem("weights_b")
        w0_added = sem("w0_added")
        idx_loaded = sem("idx_loaded")
        rows_gathered = sem("rows_gathered")
        rows_spread = sem("rows_spread")
        turned_made = sem("turned_made")
        x0_rot_made = sem("x0_rot_made")
        squares_made = sem("squares_made")
        x0_staged = sem("x0_staged")
        x0_loaded = [sem(f"x0_loaded{i}") for i in range(6)]
        l0_made = sem("l0_made")
        l0_used = sem("l0_used")
        dve_made = sem("dve_made")
        dve_used = sem("dve_used")
        pool_made = sem("pool_made")
        pool_used = sem("pool_used")
        layer_done = [sem(f"layer_done{l}") for l in range(LAYERS)]
        x_ps_made = [sem(f"x_ps_made{l}") for l in range(2)]
        x_sb_made = [sem(f"x_sb_made{l}") for l in range(2)]
        layer_out_made = sem("layer_out_made")
        z_made = [sem(f"z_made{l}") for l in range(LAYERS)]
        mlp_loaded = sem("mlp_loaded")
        dense_turned = sem("dense_turned")
        dense_made = sem("dense_made")
        mlp_done = sem("mlp_done")
        h1_made = sem("h1_made")
        h2_made = sem("h2_made")
        y_made = sem("y_made")
        y_written = sem("y_written")

        def out_count(layer, p):
            if layer == 0:
                return 1 if isinstance(p, int) and p == 0 else 3 * p
            if isinstance(p, int) and p == PAIRS - 1:
                return 3 * p + (2 if layer == 1 else 3)
            return 3 * p + (2 if layer == 1 else 4)

        def block_slot(h, block):
            return 2 * h + block if block < 2 else 2 + block

        def block_loads(it, h, block):
            return 32 * (it + 1) if block < 2 else 32 * (2 * it + h + 1)

        def x0_step(h, t):
            return x0_wide[:, block_slot(h, t // BLOCK), (t % BLOCK) * WIDE:(t % BLOCK + 1) * WIDE]

        def iterations(eng, body):
            body(0)
            with eng.Fori(1, TILES - 2) as it:
                body(it)
            body(TILES - 2)
            body(TILES - 1)

        def there(it, ahead):
            return not isinstance(it, int) or it + ahead < TILES

        block = ctx.enter_context(nc.Block())

        @block.sync
        def _(sp):
            def load_idx(tile):
                sp.dma_start(idx[:], ids[bass.ts(tile, P), :]).then_inc(idx_loaded, 16)

            def stage(p, h):
                sp.wait_ge(x0_rot_made, 2 * p + 2)
                sp.dma_start(x0_rows[h], x0_rot[0:FIELDS, :]).then_inc(x0_staged, 16)

            def load_block(h, blk):
                slot = block_slot(h, blk)
                rows = x0_rows[h].rearrange("(t a) n -> a t n", a=2)
                for a in range(2):
                    dst = x0_wide[a * HK:(a + 1) * HK, slot, :].rearrange("p (t n) -> p t n", n=WIDE)
                    src = rows[a, blk * BLOCK:(blk + 1) * BLOCK, :].unsqueeze(0).broadcast_to([HK, BLOCK, WIDE])
                    sp.dma_start(dst, src).then_inc(x0_loaded[slot], 16)

            def block_read(p, blk):
                sp.wait_ge(dve_made, 2 * N_DVE * p + N_DVE + before(DVE_STEPS, blk))
                sp.nop(nofuse=True)
                sp.wait_ge(pool_made, 2 * N_POOL * p + N_POOL + before(POOL_STEPS, blk))

            load_idx(0)
            sp.dma_start(ident_sb[:], ident).then_inc(weights, 16)
            sp.dma_start(w0_sb[:], w0_ab).then_inc(weights, 16)
            sp.dma_start(w0d_sb[:], w0_diag).then_inc(weights, 16)
            sp.dma_start(w_sb[0][:], w1.rearrange("m h k -> (m h) k").rearrange("(t p) k -> p t k", p=P)).then_inc(weights, 16)
            sp.dma_start(w_sb[1][:], w2.rearrange("m h k -> (m h) k").rearrange("(t p) k -> p t k", p=P)).then_inc(weights, 16)
            sp.dma_start(w0b_sb[:], w0_ba).then_inc(weights_b, 16)
            sp.wait_ge(rows_gathered, 16 * FIELDS)
            load_idx(1)
            stage(0, 0)
            sp.wait_ge(x0_staged, 16)
            for blk in range(BLOCKS):
                load_block(0, blk)
            stage(1, 1)
            sp.wait_ge(x0_staged, 32)
            load_block(1, 0)
            load_block(1, 1)

            def body(it):
                for h in range(2):
                    p = 2 * it + h
                    if there(it, 1):
                        stage(p + 2, h)
                    if h == 0 and there(it, 2):
                        sp.wait_ge(rows_gathered, 16 * FIELDS * (it + 2))
                        load_idx(it + 2)
                    if h == 0 or there(it, 1):
                        for blk in (2, 3):
                            block_read(p, blk)
                            load_block(1 - h, blk)
                    if there(it, 1):
                        for blk in (0, 1):
                            if blk == 0:
                                sp.wait_ge(x0_staged, 16 * (p + 3))
                                sp.nop(nofuse=True)
                            block_read(p, blk)
                            load_block(h, blk)

            iterations(sp, body)
            for l in range(LAYERS):
                for a in range(2):
                    sp.dma_start(wt1[a * HK:(a + 1) * HK, l, :], w_top1[l * HK:(l + 1) * HK, :]).then_inc(mlp_loaded, 16)
            sp.dma_start(wt1d, w_top1[LAYERS * HK:, :]).then_inc(mlp_loaded, 16)
            sp.dma_start(wt2, w_top2.rearrange("(c p) j -> p c j", p=P)).then_inc(mlp_loaded, 16)
            sp.dma_start(wt3, w_top3).then_inc(mlp_loaded, 16)
            sp.dma_start(b1, b_top1).then_inc(mlp_loaded, 16)
            sp.dma_start(b2, b_top2).then_inc(mlp_loaded, 16)
            sp.dma_start(dense, dense_ctx.rearrange("(t p) f -> p t f", p=P)).then_inc(mlp_loaded, 16)
            sp.wait_ge(y_made, BATCH // HALF)
            sp.dma_start(out.rearrange("n a -> a n"), y_sb).then_inc(y_written, 16)
            sp.wait_ge(y_written, 16)

        MLP_LOADS = 16 * (2 * LAYERS + 6)

        @block.gpsimd
        def _(pool):
            def gather(fields):
                for f in fields:
                    pool.indirect_dma_start(
                        gathered[:, f * DIM:(f + 1) * DIM], None, tables[f],
                        bass.IndirectOffsetOnAxis(ap=idx[:, f:f + 1], axis=0)).then_inc(rows_gathered, 16)

            def products(it, h, layer):
                p = 2 * it + h
                for i, t in enumerate(POOL_STEPS):
                    n = 2 * N_POOL * p + (layer - 1) * N_POOL + i
                    if i == 0:
                        pool.wait_ge(x_sb_made[layer - 1], 4 * p + 4)
                    if layer == 1:
                        pool.wait_ge(x0_loaded[block_slot(h, t // BLOCK)], block_loads(it, h, t // BLOCK))
                    if not isinstance(n, int) or n >= POOL_RING:
                        pool.wait_ge(pool_used, n - POOL_RING + 1)
                    slot = ((layer - 1) * N_POOL + i) % POOL_RING
                    nc.gpsimd.tensor_tensor(pool_ring[:, slot, :], x0_step(h, t), x_sb[layer - 1][:],
                                            ALU.mult).then_inc(pool_made, 1)

            pool.wait_ge(idx_loaded, 16)
            gather(range(FIELDS))
            pool.wait_ge(idx_loaded, 32)
            pool.wait_ge(rows_spread, 2)
            gather(range(FIELDS))

            def body(it):
                products(it, 0, 1)
                products(it, 0, 2)
                if there(it, 2):
                    pool.wait_ge(idx_loaded, 16 * (it + 3))
                    pool.wait_ge(rows_spread, 3 * (it + 1) + 2)
                    pool.nop(nofuse=True)
                    gather(range(0, 8))
                products(it, 1, 1)
                if there(it, 2):
                    gather(range(8, 20))
                products(it, 1, 2)
                if there(it, 2):
                    gather(range(20, FIELDS))

            iterations(pool, body)

        @block.scalar
        def _(act):
            def spread_rows(tile):
                act.wait_ge(rows_gathered, 16 * FIELDS * (tile + 1))
                if not isinstance(tile, int) or tile > 0:
                    act.wait_ge(turned_made, 20 * tile)
                whole = repeated[:, 0:Q * ROWS].rearrange("p (q n) -> p q n", q=Q)
                nc.scalar.copy(whole, gathered[:].unsqueeze(1).broadcast_to([P, Q, ROWS])).then_inc(rows_spread, 1)
                nc.scalar.copy(repeated[:, Q * ROWS:], gathered[:, 0:(WRAP - P) * DIM]).then_inc(rows_spread, 1)
                act.wait_ge(rows_spread, 3 * tile + 2)
                flat = repeated[:]
                windows = bass.AP(flat.tensor, flat.offset, [list(flat.ap[0]), [DIM, Q], [1, ROWS]])
                nc.scalar.copy(rotated[:].rearrange("p (q n) -> p q n", q=Q), windows).then_inc(rows_spread, 1)

            def take_x0(p):
                for c in range(2):
                    act.wait_ge(turned_made, 10 * p + c + 1)
                    if c == 0 and (not isinstance(p, int) or p > 0):
                        act.wait_ge(l0_made, L0_UNITS * p)
                        act.wait_ge(x0_staged, 16 * p)
                        act.wait_ge(layer_done[0], p)
                    nc.scalar.copy(x0_rot[:, c * CHUNK:(c + 1) * CHUNK], turned[:, c, :]).then_inc(x0_rot_made, 1)
                act.wait_ge(x0_rot_made, 2 * p + 2)
                nc.scalar.activation(squares[:], x0_rot[0:FIELDS, :], ACT.Square).then_inc(squares_made, 1)

            def finish(layer, p, h, tile):
                a = acc[h]
                act.wait_ge(layer_done[layer], p + 1)
                if layer < 2:
                    for x, made in ((x_ps[layer], x_ps_made[layer]), (x_sb[layer], x_sb_made[layer])):
                        for c in range(2):
                            for half in range(2):
                                nc.scalar.activation(x[half * HK:(half + 1) * HK, c * CHUNK:(c + 1) * CHUNK],
                                                     a[c * HK:(c + 1) * HK, :], ACT.Relu).then_inc(made, 1)
                if not isinstance(tile, int) or tile > 0:
                    act.wait_ge(z_made[layer], tile)
                nc.scalar.activation(layer_out[:, layer, h, :], a[:], ACT.Relu).then_inc(layer_out_made, 1)

            spread_rows(0)
            take_x0(0)
            finish(0, 0, 0, 0)
            take_x0(1)

            def body(it):
                for h in range(2):
                    p = 2 * it + h
                    finish(1, p, h, it)
                    if h == 0:
                        finish(0, p + 1, 1, it)
                        if there(it, 1):
                            spread_rows(it + 1)
                    elif there(it, 1):
                        finish(0, p + 1, 0, it + 1)
                    if there(it, 1):
                        take_x0(p + 2)
                    finish(2, p, h, it)

            iterations(act, body)
            act.wait_ge(dense_turned, 1)
            nc.scalar.copy(dense_t, turned[0:DIM, :, :].rearrange("p a n -> p (a n)")).then_inc(dense_made, 1)
            done = 0
            for width, bias, dst, made in ((H1, b1, h1, h1_made), (H2, b2, h2, h2_made)):
                for n in range(BATCH // HALF):
                    for j in range(width // P):
                        bank = x_ps[done % 4 // 2][:, done % 2 * CHUNK:(done % 2 + 1) * CHUNK]
                        done += 1
                        act.wait_ge(mlp_done, done)
                        nc.scalar.activation(dst[:, j, n * HALF:(n + 1) * HALF], bank, ACT.Relu,
                                             bias=bias[:, j:j + 1]).then_inc(made, 1)
            for n in range(BATCH // HALF):
                done += 1
                act.wait_ge(mlp_done, done)
                nc.scalar.copy(y_sb[:, n * HALF:(n + 1) * HALF], acc[n][0:1, :]).then_inc(y_made, 1)

        @block.vector
        def _(dve):
            def products(it, h, layer, summed=None):
                p = 2 * it + h
                for i, t in enumerate(DVE_STEPS):
                    n = 2 * N_DVE * p + (layer - 1) * N_DVE + i
                    if i == 0:
                        dve.wait_ge(x_ps_made[layer - 1], 4 * p + 4)
                    if layer == 1 and t % BLOCK == 0:
                        dve.wait_ge(x0_loaded[block_slot(h, t // BLOCK)], block_loads(it, h, t // BLOCK))
                    if not isinstance(n, int) or n >= DVE_RING:
                        dve.wait_ge(dve_used, n - DVE_RING + 1)
                    slot = ((layer - 1) * N_DVE + i) % DVE_RING
                    nc.vector.tensor_tensor(dve_ring[:, slot, :], x0_step(h, t), x_ps[layer - 1][:],
                                            ALU.mult).then_inc(dve_made, 1)
                    if i == Z_STEP and summed is not None:
                        sum_over_d(*summed)

            def sum_over_d(layer, tile):
                dve.wait_ge(layer_out_made, out_count(layer, 2 * tile + 1))
                nc.vector.tensor_reduce(z[:, layer, bass.ts(tile, P)],
                                        layer_out[:, layer].rearrange("p h (d b) -> p b (h d)", b=P),
                                        AX_X, ALU.add).then_inc(z_made[layer], 1)

            def l0_products(p):
                for u in range(L0_UNITS):
                    dve.wait_ge(turned_made, 10 * p + 3 + u)
                    if u == 0:
                        dve.wait_ge(x0_rot_made, 2 * p + 2)
                    n = L0_UNITS * p + u
                    if not isinstance(n, int) or n >= L0_RING:
                        dve.wait_ge(l0_used, n - L0_RING + 1)
                    c = u % 2
                    nc.vector.tensor_tensor(l0_ring[:, u % L0_RING, :], x0_rot[:, c * CHUNK:(c + 1) * CHUNK],
                                            turned[:, c, :], ALU.mult).then_inc(l0_made, 1)

            dve.wait_ge(weights, 80)
            dve.wait_ge(weights_b, 16)
            nc.vector.tensor_tensor(w0_sb[:, 0:SHIFT_TILES - 1, :], w0_sb[:, 0:SHIFT_TILES - 1, :],
                                    w0b_sb[:, 0:SHIFT_TILES - 1, :], ALU.add).then_inc(w0_added, 1)
            for q in range(1, Q):
                rows = slice(q * FIELDS, (q + 1) * FIELDS)
                nc.vector.tensor_tensor(w0_sb[rows, SHIFT_TILES - 1, :], w0_sb[rows, SHIFT_TILES - 1, :],
                                        w0b_sb[rows, SHIFT_TILES - 1, :], ALU.add).then_inc(w0_added, 1)
            l0_products(0)

            def body(it):
                first = isinstance(it, int) and it == 0
                products(it, 0, 1, None if first else (2, it - 1))
                l0_products(2 * it + 1)
                products(it, 0, 2, (0, it))
                products(it, 1, 1)
                if there(it, 1):
                    l0_products(2 * it + 2)
                products(it, 1, 2, (1, it))

            iterations(dve, body)
            sum_over_d(2, TILES - 1)

        @block.tensor
        def _(pe):
            repeated_v = repeated[:].rearrange("p (f d) -> p d f", d=DIM)
            rotated_v = rotated[:].rearrange("p (f d) -> p d f", d=DIM)

            def turn(rows, first, h, c):
                for i in range(D_CHUNK):
                    d = 2 * D_CHUNK * h + D_CHUNK * c + i
                    last = nc.tensor.transpose(turned[:, c, i * P:(i + 1) * P], rows[:, d, first:first + P],
                                               ident_sb[:])
                last.then_inc(turned_made, 1)

            def turn_rotated(p, h, tile):
                if h == 0:
                    pe.wait_ge(rows_spread, 3 * (tile + 1))
                for c in range(2):
                    if not isinstance(p, int) or p > 0:
                        pe.wait_ge(l0_made, L0_UNITS * p - 1 + c)
                    turn(rotated_v, 0, h, c)

            def turn_shifted(p, h, u):
                c, t = u % 2, u // 2
                if t == 0:
                    pe.wait_ge(x0_rot_made, 2 * p + c + 1)
                else:
                    pe.wait_ge(l0_made, L0_UNITS * p + u - 1)
                turn(repeated_v, Q * (t + 1), h, c)

            def l0_contract(p, h, u):
                c, t = u % 2, u // 2
                pe.wait_ge(l0_made, L0_UNITS * p + u + 1)
                last = nc.tensor.matmul(acc[h][c * HK:(c + 1) * HK, :], w0_sb[:, t, :], l0_ring[:, u % L0_RING, :],
                                        start=False, stop=(t == SHIFT_TILES - 1))
                last.then_inc(l0_used, 1)
                return last

            def layer0(p, h, first_pair=False):
                pe.wait_ge(squares_made, p + 1)
                if not first_pair:
                    pe.wait_ge(layer_out_made, 3 * p - 2)
                for c in range(2):
                    nc.tensor.matmul(acc[h][c * HK:(c + 1) * HK, :], w0d_sb[:], squares[:, c * CHUNK:(c + 1) * CHUNK],
                                     start=True, stop=False)
                for t in range(SHIFT_TILES):
                    if t + 1 < SHIFT_TILES:
                        turn_shifted(p, h, 2 * t + 2)
                        turn_shifted(p, h, 2 * t + 3)
                    l0_contract(p, h, 2 * t)
                    last = l0_contract(p, h, 2 * t + 1)
                return last

            def contract(it, h, layer, between):
                p = 2 * it + h
                pe.wait_ge(layer_out_made, out_count(layer - 1, p))
                i_dve = i_pool = 0
                for t in range(STEPS):
                    if t in POOL_STEPS:
                        at = (layer - 1) * N_POOL + i_pool
                        pe.wait_ge(pool_made, 2 * N_POOL * p + at + 1)
                        tile, used = pool_ring[:, at % POOL_RING, :], pool_used
                        i_pool += 1
                    else:
                        at = (layer - 1) * N_DVE + i_dve
                        pe.wait_ge(dve_made, 2 * N_DVE * p + at + 1)
                        tile, used = dve_ring[:, at % DVE_RING, :], dve_used
                        i_dve += 1
                    for c in range(2):
                        last = nc.tensor.matmul(acc[h][c * HK:(c + 1) * HK, :], w_sb[layer - 1][:, t, :],
                                                tile[:, c * CHUNK:(c + 1) * CHUNK],
                                                start=(t == 0), stop=(t == STEPS - 1))
                    last.then_inc(used, 1)
                    if t == STEPS - 1:
                        pe.wait_ge(used, 2 * (N_POOL if t in POOL_STEPS else N_DVE) * p + at + 1)
                        pe.sem_inc(layer_done[layer], 1)
                    if t in between:
                        between[t]()

            def finish_layer0(p):
                pe.wait_ge(l0_used, L0_UNITS * (p + 1))
                pe.sem_inc(layer_done[0], 1)

            pe.wait_ge(weights, 80)
            turn_rotated(0, 0, 0)
            turn_shifted(0, 0, 0)
            turn_shifted(0, 0, 1)
            pe.wait_ge(w0_added, Q)
            layer0(0, 0, first_pair=True)
            finish_layer0(0)
            turn_rotated(1, 1, 0)

            def body(it):
                for h in range(2):
                    p = 2 * it + h
                    ahead = h == 0 or there(it, 1)
                    early = {12: lambda: turn_shifted(p + 1, 1 - h, 0), 13: lambda: turn_shifted(p + 1, 1 - h, 1)}
                    contract(it, h, 1, early if ahead else {})
                    if ahead:
                        layer0(p + 1, 1 - h)
                        finish_layer0(p + 1)
                    contract(it, h, 2, {8: lambda: turn_rotated(p + 2, h, it + 1)} if there(it, 1) else {})

            iterations(pe, body)

            pe.wait_ge(mlp_loaded, MLP_LOADS)
            for t in range(TILES):
                last = nc.tensor.matmul(turned[0:DIM, t // D_CHUNK, t % D_CHUNK * P:(t % D_CHUNK + 1) * P],
                                        dense[:, t, :], ident_sb[:], start=True, stop=True)
            last.then_inc(dense_turned, 1)
            for l in range(LAYERS):
                pe.wait_ge(z_made[l], TILES)
            done = 0
            for n in range(BATCH // HALF):
                cols = slice(n * HALF, (n + 1) * HALF)
                for j in range(H1 // P):
                    out_cols = slice(j * P, (j + 1) * P)
                    bank = x_ps[done % 4 // 2][:, done % 2 * CHUNK:(done % 2 + 1) * CHUNK]
                    if done >= 4:
                        pe.wait_ge(h1_made, done - 3)
                    for l in range(LAYERS):
                        nc.tensor.matmul(bank, wt1[:, l, out_cols], z[:, l, cols], start=(l == 0), stop=False)
                    if done == 0:
                        pe.wait_ge(dense_made, 1)
                    nc.tensor.matmul(bank, wt1d[:, out_cols], dense_t[:, cols], start=False, stop=True)\
                        .then_inc(mlp_done, 1)
                    done += 1
            for n in range(BATCH // HALF):
                cols = slice(n * HALF, (n + 1) * HALF)
                pe.wait_ge(h1_made, H1 // P * (n + 1) if n else 8 - 4)
                for j in range(H2 // P):
                    bank = x_ps[done % 4 // 2][:, done % 2 * CHUNK:(done % 2 + 1) * CHUNK]
                    if done - 3 <= 8:
                        pe.wait_ge(h1_made, done - 3)
                    for c in range(H1 // P):
                        last = nc.tensor.matmul(bank, wt2[:, c, j * P:(j + 1) * P], h1[:, c, cols],
                                                start=(c == 0), stop=(c == H1 // P - 1))
                    last.then_inc(mlp_done, 1)
                    done += 1
            for n in range(BATCH // HALF):
                cols = slice(n * HALF, (n + 1) * HALF)
                pe.wait_ge(h2_made, H2 // P * (n + 1))
                for c in range(H2 // P):
                    last = nc.tensor.matmul(acc[n][0:1, :], wt3[:, c:c + 1], h2[:, c, cols],
                                            start=(c == 0), stop=(c == H2 // P - 1))
                last.then_inc(mlp_done, 1)


def kernel(**inputs):
    import numpy as np
    import concourse.bacc as bacc
    from concourse.bass_utils import run_bass_kernel_spmd

    w0 = np.asarray(inputs["L0_rec_W0"])
    q, m, t = np.meshgrid(np.arange(Q), np.arange(FIELDS), np.arange(SHIFT_TILES), indexing="ij")
    a = ((m + q) % FIELDS).reshape(P, SHIFT_TILES)
    b = ((m + Q * (t + 1)) % FIELDS).reshape(P, SHIFT_TILES)
    arrays = {"w0_ab": w0[a, b], "w0_ba": w0[b, a], "w0_diag": w0[np.arange(FIELDS), np.arange(FIELDS)],
              "ident": np.eye(P, dtype=np.float32)}
    for name in ("b_top1", "b_top2", "W_top3"):
        arrays[name] = np.asarray(inputs[name]).reshape(-1, P).T
    for name in ["dense_ctx", "ids", "W_top1", "W_top2", "L0_rec_W1", "L0_rec_W2"] + \
            [f"tbl_{f}" for f in range(FIELDS)]:
        arrays[name] = np.asarray(inputs[name])

    nc = bacc.Bacc("TRN2", target_bir_lowering=False, num_devices=1)
    ap, feed = {}, {}
    for name, value in arrays.items():
        feed[f"in_{name}"] = np.ascontiguousarray(value)
        ap[name] = nc.dram_tensor(f"in_{name}", value.shape, mybir.dt.from_np(value.dtype), kind="ExternalInput").ap()
    out = nc.dram_tensor("out_y", (BATCH, 1), F32, kind="ExternalOutput").ap()
    cin_tower(nc, ap["dense_ctx"], ap["ids"], [ap[f"tbl_{f}"] for f in range(FIELDS)], ap["W_top1"], ap["b_top1"],
              ap["W_top2"], ap["b_top2"], ap["W_top3"], ap["w0_ab"], ap["w0_ba"], ap["w0_diag"],
              ap["L0_rec_W1"], ap["L0_rec_W2"], ap["ident"], out)
    result = run_bass_kernel_spmd(nc, [feed], core_ids=[0])
    return result.results[0]["out_y"]
```

```python
from contextlib import ExitStack

import concourse.bass as bass
from concourse import mybir

F32 = mybir.dt.float32
I32 = mybir.dt.int32
ALU = mybir.AluOpType
ACT = mybir.ActivationFunctionType
AX_X = mybir.AxisListType.X

P = 128
BATCH = 1024
FIELDS = 32
DIM = 16
HK = 64
LAYERS = 3
TILES = BATCH // P
PAIRS = 2 * TILES
D_CHUNK = 4
CHUNK = D_CHUNK * P
WIDE = 2 * CHUNK
ROWS = FIELDS * DIM
STEPS = FIELDS // 2

Q = P // FIELDS
SHIFT_TILES = 4
L0_UNITS = 2 * SHIFT_TILES
WRAP = P + Q * SHIFT_TILES

POOL_STEPS = {(0, 1): (3, 7, 11, 15), (0, 2): (3, 7, 11), (1, 1): (3, 7, 11, 15), (1, 2): (3, 7, 11)}
POOL_STEPS_FIRST = {(0, 1): (), (0, 2): (), (1, 1): (7, 15), (1, 2): (5, 11)}
PHASES = tuple(POOL_STEPS)
DVE_RING, POOL_RING, L0_RING = 5, 2, 8
GATHERS = {(0, 2): range(0, 4), (1, 1): range(4, 16), (1, 2): range(16, 20), (0, 1): range(20, FIELDS)}
GATHERED_AFTER = {(0, 1): (2, 2, 2, 6), (0, 2): (0, 0, 4), (1, 1): (2, 2, 2, 6), (1, 2): (1, 1, 2)}
L0_EARLY = {4: (0, 1), 8: (2, 3)}
L0_LATE = (4, 5, 6, 7)

BLOCK = 4
BLOCKS = STEPS // BLOCK

H1, H2 = 512, 256
HALF = 512
REST = HK + DIM
MLP_LOADS = 16 * 6


def pool_steps(it, h, layer):
    first = isinstance(it, int) and it == 0
    return (POOL_STEPS_FIRST if first else POOL_STEPS)[h, layer]


def dve_steps(it, h, layer):
    return tuple(t for t in range(STEPS) if t not in pool_steps(it, h, layer))


def in_tile(steps, it, h, layer):
    return sum(len(steps(it, *phase)) for phase in PHASES[:PHASES.index((h, layer))])


def made_before(steps, it, h, layer):
    whole = [sum(len(steps(i, *phase)) for phase in PHASES) for i in (0, 1)]
    if isinstance(it, int) and it == 0:
        return in_tile(steps, it, h, layer)
    return whole[1] * (it - 1) + (whole[0] + in_tile(steps, it, h, layer))


for _ring, _steps in ((DVE_RING, dve_steps), (POOL_RING, pool_steps)):
    assert all(sum(len(_steps(i, *phase)) for phase in PHASES) % _ring == 0 for i in (0, 1))


def cin_tower(nc, dense_ctx, ids, tables, w_top1, b_top1, w_top2, b_top2, w_top3,
              w0_ab, w0_ba, w0_diag, w1, w2, ident, out):
    with ExitStack() as ctx:
        def sb(name, shape, dt=F32):
            return ctx.enter_context(nc.sbuf_tensor(name, shape, dt))

        def psum(name, shape):
            return ctx.enter_context(nc.psum_tensor(name, shape, F32))

        def sem(name):
            return ctx.enter_context(nc.semaphore(name))

        x0_rows = nc.dram_tensor("x0_rows", (2, FIELDS, WIDE), F32, kind="Internal").ap()

        x0_wide = sb("x0_wide", [P, 6, BLOCK * WIDE])
        dve_ring = sb("dve_ring", [P, DVE_RING, WIDE])
        pool_ring = sb("pool_ring", [P, POOL_RING, WIDE])
        l0_ring = sb("l0_ring", [P, L0_RING, CHUNK])
        gathered = sb("gathered", [P, ROWS])
        repeated = sb("repeated", [P, WRAP * DIM])
        rotated = sb("rotated", [P, P * DIM])
        x0_rot = sb("x0_rot", [P, WIDE])
        squares = sb("squares", [FIELDS, WIDE])
        x_sb = [sb(f"x_sb{l}", [P, WIDE]) for l in range(2)]
        layer_out = sb("layer_out", [P, LAYERS, 2, CHUNK])
        z_half = sb("z_half", [P, P])
        z_low = sb("z_low", [HK, P])
        features = sb("features", [P, 2, BATCH])
        w0_sb = sb("w0_sb", [P, SHIFT_TILES, HK])
        w0b_sb = sb("w0b_sb", [P, SHIFT_TILES, HK])
        w0d_sb = sb("w0d_sb", [FIELDS, HK])
        w_sb = [sb(f"w_sb{l}", [P, STEPS, HK]) for l in (1, 2)]
        ident_sb = sb("ident_sb", [P, P])
        idx = sb("idx", [P, FIELDS], I32)
        dense = sb("dense", [P, TILES, DIM])

        acc = [psum(f"acc{i}", [P, CHUNK]) for i in range(2)]
        x_ps = [psum(f"x_ps{l}", [P, WIDE]) for l in range(2)]
        turned = psum("turned", [P, 2, CHUNK])

        free0 = x0_wide[:, 0:2, :].rearrange("p a n -> p (a n)")
        free1 = x0_wide[:, 2:4, :].rearrange("p a n -> p (a n)")
        taken = [0]

        def mlp(n, rows=P):
            taken[0] += n
            return free0[0:rows, taken[0] - n:taken[0]]

        wt1 = mlp(2 * H1).rearrange("p (c j) -> p c j", c=2)
        wt2 = mlp(H1 // P * H2).rearrange("p (c j) -> p c j", j=H2)
        wt3 = mlp(H2 // P)
        b1 = mlp(H1 // P)
        b2 = mlp(H2 // P)
        y_sb = mlp(BATCH, 1)
        h1 = free1[:, 0:H1 // P * BATCH].rearrange("p (c n) -> p c n", n=BATCH)
        h2 = free1[:, H1 // P * BATCH:(H1 + H2) // P * BATCH].rearrange("p (c n) -> p c n", n=BATCH)

        weights = sem("weights")
        weights_b = sem("weights_b")
        w0_added = sem("w0_added")
        idx_loaded = sem("idx_loaded")
        rows_gathered = sem("rows_gathered")
        rows_spread = sem("rows_spread")
        turned_made = sem("turned_made")
        x0_rot_made = sem("x0_rot_made")
        squares_made = sem("squares_made")
        x0_staged = sem("x0_staged")
        x0_loaded = [sem(f"x0_loaded{i}") for i in range(6)]
        l0_made = sem("l0_made")
        l0_used = sem("l0_used")
        dve_made = sem("dve_made")
        dve_used = sem("dve_used")
        pool_made = sem("pool_made")
        pool_used = sem("pool_used")
        layer_done = [sem(f"layer_done{l}") for l in range(LAYERS)]
        x_ps_made = [sem(f"x_ps_made{l}") for l in range(2)]
        x_sb_made = [sem(f"x_sb_made{l}") for l in range(2)]
        layer_out_made = sem("layer_out_made")
        z_half_made = sem("z_half_made")
        z_low_made = sem("z_low_made")
        z_made = sem("z_made")
        dense_loaded = sem("dense_loaded")
        mlp_loaded = sem("mlp_loaded")
        dense_turned = sem("dense_turned")
        dense_made = sem("dense_made")
        mlp_done = sem("mlp_done")
        h1_made = sem("h1_made")
        h2_made = sem("h2_made")
        y_made = sem("y_made")
        y_written = sem("y_written")

        def out_count(layer, p):
            if layer == 0:
                return 1 if isinstance(p, int) and p == 0 else 3 * p
            if isinstance(p, int) and p == PAIRS - 1:
                return 3 * p + (2 if layer == 1 else 3)
            return 3 * p + (2 if layer == 1 else 4)

        def block_slot(h, block):
            return 2 * h + block if block < 2 else 2 + block

        def block_loads(it, h, block):
            return 32 * (it + 1) if block < 2 else 32 * (2 * it + h + 1)

        def x0_step(h, t):
            return x0_wide[:, block_slot(h, t // BLOCK), (t % BLOCK) * WIDE:(t % BLOCK + 1) * WIDE]

        def iterations(eng, body):
            body(0)
            with eng.Fori(1, TILES - 2) as it:
                body(it)
            body(TILES - 2)
            body(TILES - 1)

        def there(it, ahead):
            return not isinstance(it, int) or it + ahead < TILES

        block = ctx.enter_context(nc.Block())

        @block.sync
        def _(sp):
            def load_idx(tile):
                sp.dma_start(idx[:], ids[bass.ts(tile, P), :]).then_inc(idx_loaded, 16)

            def stage(p, h):
                sp.wait_ge(x0_rot_made, 2 * p + 2)
                sp.dma_start(x0_rows[h], x0_rot[0:FIELDS, :]).then_inc(x0_staged, 16)

            def load_block(h, blk):
                slot = block_slot(h, blk)
                rows = x0_rows[h].rearrange("(t a) n -> a t n", a=2)
                for a in range(2):
                    dst = x0_wide[a * HK:(a + 1) * HK, slot, :].rearrange("p (t n) -> p t n", n=WIDE)
                    src = rows[a, blk * BLOCK:(blk + 1) * BLOCK, :].unsqueeze(0).broadcast_to([HK, BLOCK, WIDE])
                    sp.dma_start(dst, src).then_inc(x0_loaded[slot], 16)

            def block_read(it, h, blk):
                def through(steps):
                    return made_before(steps, it, h, 2) + sum(t < BLOCK * (blk + 1) for t in steps(it, h, 2))

                sp.wait_ge(dve_made, through(dve_steps))
                sp.nop(nofuse=True)
                if not isinstance(it, int) or through(pool_steps) > 0:
                    sp.wait_ge(pool_made, through(pool_steps))

            load_idx(0)
            sp.dma_start(dense[:], dense_ctx.rearrange("(t p) f -> p t f", p=P)).then_inc(dense_loaded, 16)
            sp.dma_start(ident_sb[:], ident).then_inc(weights, 16)
            sp.dma_start(w0_sb[:], w0_ab).then_inc(weights, 16)
            sp.dma_start(w0d_sb[:], w0_diag).then_inc(weights, 16)
            sp.dma_start(w_sb[0][:], w1.rearrange("m h k -> (m h) k").rearrange("(t p) k -> p t k", p=P)).then_inc(weights, 16)
            sp.dma_start(w_sb[1][:], w2.rearrange("m h k -> (m h) k").rearrange("(t p) k -> p t k", p=P)).then_inc(weights, 16)
            sp.dma_start(w0b_sb[:], w0_ba).then_inc(weights_b, 16)
            sp.wait_ge(rows_gathered, 16 * FIELDS)
            load_idx(1)
            stage(0, 0)
            sp.wait_ge(x0_staged, 16)
            for blk in range(BLOCKS):
                load_block(0, blk)
            stage(1, 1)
            sp.wait_ge(x0_staged, 32)
            load_block(1, 0)
            load_block(1, 1)

            def body(it):
                for h in range(2):
                    p = 2 * it + h
                    if h == 0 and there(it, 2):
                        sp.wait_ge(rows_gathered, 16 * FIELDS * (it + 2))
                        load_idx(it + 2)
                    if there(it, 1):
                        stage(p + 2, h)
                    if h == 0 or there(it, 1):
                        for blk in (2, 3):
                            block_read(it, h, blk)
                            load_block(1 - h, blk)
                    if there(it, 1):
                        for blk in (0, 1):
                            if blk == 0:
                                sp.wait_ge(x0_staged, 16 * (p + 3))
                                sp.nop(nofuse=True)
                            block_read(it, h, blk)
                            load_block(h, blk)

            iterations(sp, body)
            sp.dma_start(wt1[:, 0, :], w_top1[0:P, :]).then_inc(mlp_loaded, 16)
            sp.dma_start(wt1[0:REST, 1, :], w_top1[P:, :]).then_inc(mlp_loaded, 16)
            sp.dma_start(wt2, w_top2.rearrange("(c p) j -> p c j", p=P)).then_inc(mlp_loaded, 16)
            sp.dma_start(wt3, w_top3).then_inc(mlp_loaded, 16)
            sp.dma_start(b1, b_top1).then_inc(mlp_loaded, 16)
            sp.dma_start(b2, b_top2).then_inc(mlp_loaded, 16)
            sp.wait_ge(y_made, BATCH // HALF)
            sp.dma_start(out.rearrange("n a -> a n"), y_sb).then_inc(y_written, 16)
            sp.wait_ge(y_written, 16)

        @block.gpsimd
        def _(pool):
            def gather(fields):
                for f in fields:
                    pool.indirect_dma_start(
                        gathered[:, f * DIM:(f + 1) * DIM], None, tables[f],
                        bass.IndirectOffsetOnAxis(ap=idx[:, f:f + 1], axis=0)).then_inc(rows_gathered, 16)

            def phase(it, h, layer):
                p = 2 * it + h
                steps = pool_steps(it, h, layer)
                first = isinstance(it, int) and it == 0
                fields = list(GATHERS[h, layer])
                if not there(it, 1 if (h, layer) == (0, 1) else 2) or (first and (h, layer) == (0, 1)):
                    fields = []
                late = (h, layer) == (0, 2)
                for i, t in enumerate(steps):
                    n = made_before(pool_steps, it, h, layer) + i
                    if i == 0:
                        pool.wait_ge(x_sb_made[layer - 1], 4 * p + 4)
                    if layer == 1:
                        pool.wait_ge(x0_loaded[block_slot(h, t // BLOCK)], block_loads(it, h, t // BLOCK))
                    if not isinstance(n, int) or n >= POOL_RING:
                        pool.wait_ge(pool_used, n - POOL_RING + 1)
                    slot = (in_tile(pool_steps, it, h, layer) + i) % POOL_RING
                    nc.gpsimd.tensor_tensor(pool_ring[:, slot, :], x0_step(h, t), x_sb[layer - 1][:],
                                            ALU.mult).then_inc(pool_made, 1)
                    if not late and len(steps) == len(GATHERED_AFTER[h, layer]):
                        share = GATHERED_AFTER[h, layer][i]
                        gather(fields[:share])
                        fields = fields[share:]
                if fields and late:
                    pool.wait_ge(idx_loaded, 16 * (it + 3))
                    pool.wait_ge(rows_spread, 3 * (it + 1) + 2)
                    pool.nop(nofuse=True)
                gather(fields)

            pool.wait_ge(idx_loaded, 16)
            gather(range(FIELDS))
            pool.wait_ge(idx_loaded, 32)
            pool.wait_ge(rows_spread, 2)
            gather(range(FIELDS))

            def body(it):
                for h, layer in PHASES:
                    phase(it, h, layer)

            iterations(pool, body)

        @block.scalar
        def _(act):
            def spread_rows(tile):
                act.wait_ge(rows_gathered, 16 * FIELDS * (tile + 1))
                if not isinstance(tile, int) or tile > 0:
                    act.wait_ge(turned_made, 20 * tile)
                whole = repeated[:, 0:Q * ROWS].rearrange("p (q n) -> p q n", q=Q)
                nc.scalar.copy(whole, gathered[:].unsqueeze(1).broadcast_to([P, Q, ROWS])).then_inc(rows_spread, 1)
                nc.scalar.copy(repeated[:, Q * ROWS:], gathered[:, 0:(WRAP - P) * DIM]).then_inc(rows_spread, 1)
                act.wait_ge(rows_spread, 3 * tile + 2)
                flat = repeated[:]
                windows = bass.AP(flat.tensor, flat.offset, [list(flat.ap[0]), [DIM, Q], [1, ROWS]])
                nc.scalar.copy(rotated[:].rearrange("p (q n) -> p q n", q=Q), windows).then_inc(rows_spread, 1)

            def take_x0(p):
                for c in range(2):
                    act.wait_ge(turned_made, 10 * p + c + 1)
                    if c == 0 and (not isinstance(p, int) or p > 0):
                        act.wait_ge(l0_made, L0_UNITS * p)
                        act.wait_ge(x0_staged, 16 * p)
                        act.wait_ge(layer_done[0], p)
                    nc.scalar.copy(x0_rot[:, c * CHUNK:(c + 1) * CHUNK], turned[:, c, :]).then_inc(x0_rot_made, 1)
                act.wait_ge(x0_rot_made, 2 * p + 2)
                nc.scalar.activation(squares[:], x0_rot[0:FIELDS, :], ACT.Square).then_inc(squares_made, 1)

            def finish(layer, p, h, tile):
                a = acc[h]
                act.wait_ge(layer_done[layer], p + 1)

                if layer < 2:
                    for c in range(2):
                        for half in range(2):
                            nc.scalar.activation(x_ps[layer][half * HK:(half + 1) * HK, c * CHUNK:(c + 1) * CHUNK],
                                                 a[c * HK:(c + 1) * HK, :], ACT.Relu).then_inc(x_ps_made[layer], 1)
                if not isinstance(tile, int) or tile > 0:
                    act.wait_ge(z_half_made, LAYERS * (tile - 1) + (layer + 1))
                nc.scalar.activation(layer_out[:, layer, h, :], a[:], ACT.Relu).then_inc(layer_out_made, 1)
                if layer < 2:
                    act.wait_ge(layer_out_made, out_count(layer, p))
                    for c in range(2):
                        for half in range(2):
                            nc.scalar.copy(x_sb[layer][half * HK:(half + 1) * HK, c * CHUNK:(c + 1) * CHUNK],
                                           layer_out[c * HK:(c + 1) * HK, layer, h, :]).then_inc(x_sb_made[layer], 1)

            def lower(layer, tile):
                act.wait_ge(z_half_made, LAYERS * tile + (layer + 1))
                if not isinstance(tile, int) or tile + layer > 0:
                    act.wait_ge(z_made, LAYERS * tile + layer)
                nc.scalar.copy(z_low[:], z_half[HK:P, :]).then_inc(z_low_made, 1)

            act.wait_ge(dense_turned, 1)
            for c in range(2):
                nc.scalar.copy(features[HK:REST, 1, c * CHUNK:(c + 1) * CHUNK],
                               turned[0:DIM, c, :]).then_inc(dense_made, 1)
            spread_rows(0)
            take_x0(0)
            finish(0, 0, 0, 0)
            take_x0(1)

            def body(it):
                for h in range(2):
                    p = 2 * it + h
                    finish(1, p, h, it)
                    if h == 1:
                        lower(0, it)
                    elif not (isinstance(it, int) and it == 0):
                        lower(2, it - 1)
                    if h == 0:
                        finish(0, p + 1, 1, it)
                        if there(it, 1):
                            spread_rows(it + 1)
                    elif there(it, 1):
                        finish(0, p + 1, 0, it + 1)
                    if there(it, 1):
                        take_x0(p + 2)
                    if h == 1:
                        lower(1, it)
                    finish(2, p, h, it)

            iterations(act, body)
            lower(2, TILES - 1)
            done = 0
            for width, bias, dst, made in ((H1, b1, h1, h1_made), (H2, b2, h2, h2_made)):
                for n in range(BATCH // HALF):
                    for j in range(width // P):
                        bank = x_ps[done % 4 // 2][:, done % 2 * CHUNK:(done % 2 + 1) * CHUNK]
                        done += 1
                        act.wait_ge(mlp_done, done)
                        nc.scalar.activation(dst[:, j, n * HALF:(n + 1) * HALF], bank, ACT.Relu,
                                             bias=bias[:, j:j + 1]).then_inc(made, 1)
            for n in range(BATCH // HALF):
                done += 1
                act.wait_ge(mlp_done, done)
                nc.scalar.copy(y_sb[:, n * HALF:(n + 1) * HALF], acc[n][32 * n:32 * n + 1, :]).then_inc(y_made, 1)

        @block.vector
        def _(dve):
            def products(it, h, layer, between):
                p = 2 * it + h
                for i, t in enumerate(dve_steps(it, h, layer)):
                    n = made_before(dve_steps, it, h, layer) + i
                    if i == 0:
                        dve.wait_ge(x_ps_made[layer - 1], 4 * p + 4)
                    if layer == 1 and t % BLOCK == 0:
                        dve.wait_ge(x0_loaded[block_slot(h, t // BLOCK)], block_loads(it, h, t // BLOCK))
                    if not isinstance(n, int) or n >= DVE_RING:
                        dve.wait_ge(dve_used, n - DVE_RING + 1)
                    slot = (in_tile(dve_steps, it, h, layer) + i) % DVE_RING
                    nc.vector.tensor_tensor(dve_ring[:, slot, :], x0_step(h, t), x_ps[layer - 1][:],
                                            ALU.mult).then_inc(dve_made, 1)
                    if i + 1 in between:
                        between[i + 1]()

            def sum_over_d(layer, tile):
                dve.wait_ge(layer_out_made, out_count(layer, 2 * tile + 1))
                if not isinstance(tile, int) or tile + layer > 0:
                    dve.wait_ge(z_low_made, LAYERS * tile + layer)
                    dve.wait_ge(z_made, LAYERS * tile + layer)
                nc.vector.tensor_reduce(z_half[:],
                                        layer_out[:, layer].rearrange("p h (d b) -> p b (h d)", b=P),
                                        AX_X, ALU.add).then_inc(z_half_made, 1)

            def join_chunks(layer, tile):
                rows = slice(HK, P) if layer == 1 else slice(0, HK)
                dve.wait_ge(z_low_made, LAYERS * tile + (layer + 1))
                nc.vector.tensor_tensor(features[rows, layer // 2, bass.ts(tile, P)], z_half[0:HK, :],
                                        z_low[:], ALU.add).then_inc(z_made, 1)

            def l0_products(p, units):
                for u in units:
                    dve.wait_ge(turned_made, 10 * p + 3 + u)
                    if u == 0:
                        dve.wait_ge(x0_rot_made, 2 * p + 2)
                    n = L0_UNITS * p + u
                    if not isinstance(n, int) or n >= L0_RING:
                        dve.wait_ge(l0_used, n - L0_RING + 1)
                    c = u % 2
                    nc.vector.tensor_tensor(l0_ring[:, u % L0_RING, :], x0_rot[:, c * CHUNK:(c + 1) * CHUNK],
                                            turned[:, c, :], ALU.mult).then_inc(l0_made, 1)

            dve.wait_ge(weights, 80)
            dve.wait_ge(weights_b, 16)
            nc.vector.tensor_tensor(w0_sb[:, 0:SHIFT_TILES - 1, :], w0_sb[:, 0:SHIFT_TILES - 1, :],
                                    w0b_sb[:, 0:SHIFT_TILES - 1, :], ALU.add).then_inc(w0_added, 1)
            for q in range(1, Q):
                rows = slice(q * FIELDS, (q + 1) * FIELDS)
                nc.vector.tensor_tensor(w0_sb[rows, SHIFT_TILES - 1, :], w0_sb[rows, SHIFT_TILES - 1, :],
                                        w0b_sb[rows, SHIFT_TILES - 1, :], ALU.add).then_inc(w0_added, 1)
            l0_products(0, range(L0_UNITS))

            def body(it):
                first = isinstance(it, int) and it == 0
                for h in range(2):
                    p = 2 * it + h
                    ahead = h == 0 or there(it, 1)
                    products(it, h, 1, {i: lambda units=units: l0_products(p + 1, units)
                                        for i, units in L0_EARLY.items()} if ahead else {})
                    if h == 1:
                        sum_over_d(0, it)
                    elif not first:
                        sum_over_d(2, it - 1)
                    if ahead:
                        l0_products(p + 1, L0_LATE)
                    if h == 1:
                        products(it, h, 2, {3: lambda: join_chunks(0, it), 6: lambda: sum_over_d(1, it),
                                            10: lambda: join_chunks(1, it)})
                    else:
                        products(it, h, 2, {} if first else {3: lambda: join_chunks(2, it - 1)})

            iterations(dve, body)
            sum_over_d(2, TILES - 1)
            join_chunks(2, TILES - 1)

        @block.tensor
        def _(pe):
            repeated_v = repeated[:].rearrange("p (f d) -> p d f", d=DIM)
            rotated_v = rotated[:].rearrange("p (f d) -> p d f", d=DIM)

            def turn(rows, first, h, c):
                for i in range(D_CHUNK):
                    d = 2 * D_CHUNK * h + D_CHUNK * c + i
                    last = nc.tensor.transpose(turned[:, c, i * P:(i + 1) * P], rows[:, d, first:first + P],
                                               ident_sb[:])
                last.then_inc(turned_made, 1)

            def turn_rotated(p, h, tile):
                if h == 0:
                    pe.wait_ge(rows_spread, 3 * (tile + 1))
                for c in range(2):
                    if not isinstance(p, int) or p > 0:
                        pe.wait_ge(l0_made, L0_UNITS * p - 1 + c)
                    turn(rotated_v, 0, h, c)

            def turn_shifted(p, h, u):
                c, t = u % 2, u // 2
                if t == 0:
                    pe.wait_ge(x0_rot_made, 2 * p + c + 1)
                else:
                    pe.wait_ge(l0_made, L0_UNITS * p + u - 1)
                turn(repeated_v, Q * (t + 1), h, c)

            def shifted(p, h, u):
                turn_shifted(p, h, u)
                turn_shifted(p, h, u + 1)

            def l0_contract(p, h, u):
                c, t = u % 2, u // 2
                pe.wait_ge(l0_made, L0_UNITS * p + u + 1)
                last = nc.tensor.matmul(acc[h][c * HK:(c + 1) * HK, :], w0_sb[:, t, :], l0_ring[:, u % L0_RING, :],
                                        start=(t == 0), stop=False)
                last.then_inc(l0_used, 1)

            def layer0(p, h):
                if not isinstance(p, int) or p > 1:
                    pe.wait_ge(layer_out_made, 3 * p - 2)
                for u in (0, 1, 2, 3):
                    l0_contract(p, h, u)
                for u in (6, 7):
                    turn_shifted(p, h, u)
                for u in (4, 5, 6, 7):
                    l0_contract(p, h, u)
                pe.wait_ge(squares_made, p + 1)
                for c in range(2):
                    last = nc.tensor.matmul(acc[h][c * HK:(c + 1) * HK, :], w0d_sb[:],
                                            squares[:, c * CHUNK:(c + 1) * CHUNK], start=False, stop=True)
                last.then_inc(layer_done[0], 1)

            def contract(it, h, layer, between):
                p = 2 * it + h
                pe.wait_ge(layer_out_made, out_count(layer - 1, p))
                i_dve = i_pool = 0
                for t in range(STEPS):
                    if t in pool_steps(it, h, layer):
                        pe.wait_ge(pool_made, made_before(pool_steps, it, h, layer) + i_pool + 1)
                        tile = pool_ring[:, (in_tile(pool_steps, it, h, layer) + i_pool) % POOL_RING, :]
                        used = pool_used
                        i_pool += 1
                    else:
                        pe.wait_ge(dve_made, made_before(dve_steps, it, h, layer) + i_dve + 1)
                        tile = dve_ring[:, (in_tile(dve_steps, it, h, layer) + i_dve) % DVE_RING, :]
                        used = dve_used
                        i_dve += 1
                    for c in range(2):
                        last = nc.tensor.matmul(acc[h][c * HK:(c + 1) * HK, :], w_sb[layer - 1][:, t, :],
                                                tile[:, c * CHUNK:(c + 1) * CHUNK],
                                                start=(t == 0), stop=(t == STEPS - 1))
                    last.then_inc(used, 1)
                    if t == STEPS - 1:
                        n = (i_pool if used is pool_used else i_dve)
                        steps = pool_steps if used is pool_used else dve_steps
                        pe.wait_ge(used, made_before(steps, it, h, layer) + n)
                        pe.sem_inc(layer_done[layer], 1)
                    if t in between:
                        between[t]()

            pe.wait_ge(dense_loaded, 16)
            pe.wait_ge(weights, 80)
            for t in range(TILES):
                last = nc.tensor.matmul(turned[0:DIM, t // D_CHUNK, t % D_CHUNK * P:(t % D_CHUNK + 1) * P],
                                        dense[:, t, :], ident_sb[:], start=True, stop=True)
            last.then_inc(dense_turned, 1)
            pe.wait_ge(dense_made, 2)
            turn_rotated(0, 0, 0)
            for u in range(2):
                turn_shifted(0, 0, u)
            pe.wait_ge(w0_added, Q)
            for u in (2, 3, 4, 5):
                turn_shifted(0, 0, u)
                if u == 3:
                    l0_contract(0, 0, 0)
                    l0_contract(0, 0, 1)
            for u in (6, 7):
                turn_shifted(0, 0, u)
            for u in range(2, L0_UNITS):
                l0_contract(0, 0, u)
            pe.wait_ge(squares_made, 1)
            for c in range(2):
                last = nc.tensor.matmul(acc[0][c * HK:(c + 1) * HK, :], w0d_sb[:], squares[:, c * CHUNK:(c + 1) * CHUNK],
                                        start=False, stop=True)
            last.then_inc(layer_done[0], 1)
            turn_rotated(1, 1, 0)
            shifted(1, 1, 0)

            def body(it):
                for h in range(2):
                    p = 2 * it + h
                    ahead = h == 0 or there(it, 1)

                    contract(it, h, 1, {3: lambda: shifted(p + 1, 1 - h, 2), 7: lambda: shifted(p + 1, 1 - h, 4)}
                             if ahead else {})
                    if ahead:
                        layer0(p + 1, 1 - h)
                    contract(it, h, 2, {8: lambda: turn_rotated(p + 2, h, it + 1),
                                        13: lambda: shifted(p + 2, h, 0)} if there(it, 1) else {})

            iterations(pe, body)

            pe.wait_ge(mlp_loaded, MLP_LOADS)
            done = 0
            for n in range(BATCH // HALF):
                cols = slice(n * HALF, (n + 1) * HALF)
                pe.wait_ge(z_made, LAYERS * HALF // P * (n + 1))
                for j in range(H1 // P):
                    out_cols = slice(j * P, (j + 1) * P)
                    bank = x_ps[done % 4 // 2][:, done % 2 * CHUNK:(done % 2 + 1) * CHUNK]
                    if done >= 4:
                        pe.wait_ge(h1_made, done - 3)
                    nc.tensor.matmul(bank, wt1[:, 0, out_cols], features[:, 0, cols], start=True, stop=False)
                    nc.tensor.matmul(bank, wt1[0:REST, 1, out_cols], features[0:REST, 1, cols],
                                     start=False, stop=True).then_inc(mlp_done, 1)
                    done += 1
            for n in range(BATCH // HALF):
                cols = slice(n * HALF, (n + 1) * HALF)
                pe.wait_ge(h1_made, H1 // P * (n + 1) if n else 8 - 4)
                for j in range(H2 // P):
                    bank = x_ps[done % 4 // 2][:, done % 2 * CHUNK:(done % 2 + 1) * CHUNK]
                    if done - 3 <= 8:
                        pe.wait_ge(h1_made, done - 3)
                    for c in range(H1 // P):
                        last = nc.tensor.matmul(bank, wt2[:, c, j * P:(j + 1) * P], h1[:, c, cols],
                                                start=(c == 0), stop=(c == H1 // P - 1))
                    last.then_inc(mlp_done, 1)
                    done += 1
            pe.wait_ge(h2_made, H2 // P * BATCH // HALF)
            for c in range(H2 // P):
                for n in range(BATCH // HALF):
                    last = nc.tensor.matmul(acc[n][32 * n:32 * n + 1, :], wt3[:, c:c + 1],
                                            h2[:, c, n * HALF:(n + 1) * HALF],
                                            start=(c == 0), stop=(c == H2 // P - 1))
                    if c == H2 // P - 1:
                        last.then_inc(mlp_done, 1)


def kernel(**inputs):
    import numpy as np
    import concourse.bacc as bacc
    from concourse.bass_utils import run_bass_kernel_spmd

    w0 = np.asarray(inputs["L0_rec_W0"])
    q, m, t = np.meshgrid(np.arange(Q), np.arange(FIELDS), np.arange(SHIFT_TILES), indexing="ij")
    a = ((m + q) % FIELDS).reshape(P, SHIFT_TILES)
    b = ((m + Q * (t + 1)) % FIELDS).reshape(P, SHIFT_TILES)
    arrays = {"w0_ab": w0[a, b], "w0_ba": w0[b, a], "w0_diag": w0[np.arange(FIELDS), np.arange(FIELDS)],
              "ident": np.eye(P, dtype=np.float32)}
    for name in ("b_top1", "b_top2", "W_top3"):
        arrays[name] = np.asarray(inputs[name]).reshape(-1, P).T
    for name in ["dense_ctx", "ids", "W_top1", "W_top2", "L0_rec_W1", "L0_rec_W2"] + \
            [f"tbl_{f}" for f in range(FIELDS)]:
        arrays[name] = np.asarray(inputs[name])

    nc = bacc.Bacc("TRN2", target_bir_lowering=False, num_devices=1)
    ap, feed = {}, {}
    for name, value in arrays.items():
        feed[f"in_{name}"] = np.ascontiguousarray(value)
        ap[name] = nc.dram_tensor(f"in_{name}", value.shape, mybir.dt.from_np(value.dtype), kind="ExternalInput").ap()
    out = nc.dram_tensor("out_y", (BATCH, 1), F32, kind="ExternalOutput").ap()
    cin_tower(nc, ap["dense_ctx"], ap["ids"], [ap[f"tbl_{f}"] for f in range(FIELDS)], ap["W_top1"], ap["b_top1"],
              ap["W_top2"], ap["b_top2"], ap["W_top3"], ap["w0_ab"], ap["w0_ba"], ap["w0_diag"],
              ap["L0_rec_W1"], ap["L0_rec_W2"], ap["ident"], out)
    result = run_bass_kernel_spmd(nc, [feed], core_ids=[0])
    return result.results[0]["out_y"]
```

```python
from contextlib import ExitStack

import concourse.bass as bass
from concourse import mybir

F32 = mybir.dt.float32
I32 = mybir.dt.int32
ALU = mybir.AluOpType
ACT = mybir.ActivationFunctionType
AX_X = mybir.AxisListType.X

P = 128
BATCH = 1024
FIELDS = 32
DIM = 16
HK = 64
LAYERS = 3
TILES = BATCH // P
PAIRS = 2 * TILES
D_CHUNK = 4
CHUNK = D_CHUNK * P
WIDE = 2 * CHUNK
ROWS = FIELDS * DIM
STEPS = FIELDS // 2

Q = P // FIELDS
FIRST_FIELD = 4
COPIED = FIELDS + STEPS
ROW_TILES = ROWS // P
F_TILE = FIELDS // ROW_TILES
KEPT = FIELDS + 3 * F_TILE

SHIFT_TILES = 4

POOL_STEPS = {(0, 1): (4, 9, 14), (0, 2): (5, 10, 15), (1, 1): (4, 9, 14), (1, 2): (4, 7, 10, 13, 15)}
POOL_STEPS_FIRST = {(0, 1): (), (0, 2): (6, 11), (1, 1): (4, 9, 14), (1, 2): (4, 7, 10, 13, 15)}
POOL_STEPS_LAST = {(0, 1): (3, 6, 9, 12), (0, 2): (3, 6, 9, 12, 15), (1, 1): (3, 6, 9, 12, 15), (1, 2): (3, 6, 9, 12, 15)}
PHASES = tuple(POOL_STEPS)
DVE_RING, POOL_RING = 10, 2
GATHERED = {(0, 1): (0, 3, 3, 6), (0, 2): (0, 2, 2, 4), (1, 1): (0, 3, 3, 6), (1, 2): (0, 0, 0, 0, 0, 0)}
GATHERED_FIRST = {(0, 1): (16,), (0, 2): (0, 3, 3), (1, 1): (0, 3, 3, 4), (1, 2): (0, 0, 0, 0, 0, 0)}
L0_EARLY = {1: slice(0, 1)}
L0_LATE = slice(1, SHIFT_TILES)

BLOCK = STEPS // SHIFT_TILES
FIRST_STEP = {1: 0, 2: 2 * BLOCK}

NEAR_FIRST = 3

WARM_UP = 52

H1, H2 = 512, 256
HALF = 512
REST = HK + DIM
MLP_LOADS = 16 * 6
MLP_ORDER = [(layer, n, j) for n in range(BATCH // HALF) for layer, width in ((1, H1), (2, H2))
             for j in range(width // P)]
MLP_EARLY = H1 // P


def l0_order(p):
    return (0, 1, 2, 3) if isinstance(p, int) and p < NEAR_FIRST else (0, 2, 3, 1)


def of_tile(it, first, middle, last):
    if not isinstance(it, int):
        return middle
    return first if it == 0 else last if it >= TILES - 2 else middle


def pool_steps(it, h, layer):
    return of_tile(it, POOL_STEPS_FIRST, POOL_STEPS, POOL_STEPS_LAST)[h, layer]


def dve_steps(it, h, layer):
    return tuple(t for t in range(STEPS) if t not in pool_steps(it, h, layer))


def whole(steps, it):
    return sum(len(steps(it, *phase)) for phase in PHASES)


def made_before(steps, it, h, layer):
    in_tile = sum(len(steps(it, *phase)) for phase in PHASES[:PHASES.index((h, layer))])
    if isinstance(it, int):
        return sum(whole(steps, i) for i in range(it)) + in_tile
    return whole(steps, 1) * (it - 1) + (whole(steps, 0) + in_tile)


def ring_slot(steps, ring, it, h, layer, i):
    return (made_before(steps, it if isinstance(it, int) else 1, h, layer) + i) % ring


def dve_groups(it, h, layer):
    groups = []
    for i, t in enumerate(dve_steps(it, h, layer)):
        if (i >= 6 and len(groups[-1]) == 1 and groups[-1][0] == t - 1 and t % BLOCK
                and ring_slot(dve_steps, DVE_RING, it, h, layer, i)):
            groups[-1].append(t)
        else:
            groups.append([t])
    return groups


assert whole(dve_steps, 1) % DVE_RING == 0 and whole(pool_steps, 1) % POOL_RING == 0
assert all(sum(map(sum, gathered.values())) == FIELDS for gathered in (GATHERED, GATHERED_FIRST))


def cin_tower(nc, dense_ctx, ids, tables, w_top1, b_top1, w_top2, b_top2, w_top3,
              w0_ab, w0_ba, w0_diag, two_orders, w1, w2, ident, out):
    with ExitStack() as ctx:
        def sb(name, shape, dt=F32):
            return ctx.enter_context(nc.sbuf_tensor(name, shape, dt))

        def psum(name, shape):
            return ctx.enter_context(nc.psum_tensor(name, shape, F32))

        def sem(name):
            return ctx.enter_context(nc.semaphore(name))

        x0_rows = nc.dram_tensor("x0_rows", (TILES * KEPT, DIM * P), F32, kind="Internal").ap()
        x0_copies = nc.dram_tensor("x0_copies", (TILES * 2 * COPIED * Q, WIDE), F32, kind="Internal").ap()

        x0_wide = sb("x0_wide", [P, 6, BLOCK * WIDE])
        dve_ring = sb("dve_ring", [P, DVE_RING, WIDE])
        pool_ring = sb("pool_ring", [P, POOL_RING, WIDE])
        gathered = sb("gathered", [P, ROWS])
        x0_t = sb("x0_t", [P, ROW_TILES, P])
        x0_rot = sb("x0_rot", [P, WIDE])
        l0_tiles = sb("l0_tiles", [P, SHIFT_TILES, WIDE])
        x_sb = [sb(f"x_sb{l}", [P, WIDE]) for l in range(2)]
        layer_out = sb("layer_out", [P, LAYERS, 2, CHUNK])
        z_half = sb("z_half", [P, P])
        z_low = sb("z_low", [HK, P])
        features = sb("features", [P, 2, BATCH])
        w0_sb = sb("w0_sb", [P, SHIFT_TILES, HK])
        w0d_sb = sb("w0d_sb", [P, HK])
        w_sb = [sb(f"w_sb{l}", [P, STEPS, HK]) for l in (1, 2)]
        ident_sb = sb("ident_sb", [P, P])
        idx = sb("idx", [P, TILES, FIELDS], I32)

        acc = [psum(f"acc{i}", [P, CHUNK]) for i in range(2)]
        x_ps = [psum(f"x_ps{l}", [P, WIDE]) for l in range(2)]
        x0_rot_ps = psum("x0_rot_ps", [P, WIDE])

        gathered1 = pool_ring[:, 0, 0:ROWS]
        w0b_sb = pool_ring[:, 1, 0:SHIFT_TILES * HK].rearrange("p (t k) -> p t k", k=HK)
        two_orders_sb = pool_ring[:, 1, SHIFT_TILES * HK:SHIFT_TILES * (HK + 1)]
        dense = pool_ring[:, 1, CHUNK:CHUNK + TILES * DIM].rearrange("p (t f) -> p t f", f=DIM)

        free0 = x0_wide[:, 0:2, :].rearrange("p a n -> p (a n)")
        free1 = x0_wide[:, 2, :]
        taken = [0]

        def mlp(n, rows=P):
            taken[0] += n
            return free0[0:rows, taken[0] - n:taken[0]]

        wt1 = mlp(2 * H1).rearrange("p (c j) -> p c j", c=2)
        wt2 = mlp(H1 // P * H2).rearrange("p (c j) -> p c j", j=H2)
        wt3 = mlp(H2 // P)
        b1 = mlp(H1 // P)
        b2 = mlp(H2 // P)
        y_sb = mlp(BATCH, 1)
        h1 = l0_tiles
        h2 = free1[:, 0:H2 // P * BATCH].rearrange("p (c n) -> p c n", n=BATCH)

        mlp_banks = [bank[:, c * CHUNK:(c + 1) * CHUNK] for bank in (x0_rot_ps, *x_ps) for c in range(2)]

        weights = sem("weights")
        weights_b = sem("weights_b")
        w0_added = sem("w0_added")
        idx_loaded = sem("idx_loaded")
        idx_moved = sem("idx_moved")
        first_gathered = [sem(f"first_gathered{j}") for j in range(ROW_TILES)]
        tile1_gathered = sem("tile1_gathered")
        rows_gathered = sem("rows_gathered")
        turned_made = sem("turned_made")
        x0_t_made = sem("x0_t_made")
        x0_staged = sem("x0_staged")
        rot_loaded = sem("rot_loaded")
        x0_copied = [sem(f"x0_copied{h}") for h in range(2)]
        near_loaded = [sem(f"near_loaded{p}") for p in range(NEAR_FIRST)]
        far_loaded = sem("far_loaded")
        rot_ps_made = sem("rot_ps_made")
        squares_made = sem("squares_made")
        x0_loaded = [sem(f"x0_loaded{i}") for i in range(6)]
        l0_made = sem("l0_made")
        dve_made = sem("dve_made")
        dve_used = sem("dve_used")
        pool_made = sem("pool_made")
        pool_used = sem("pool_used")
        layer0_done = sem("layer0_done")
        x_ps_made = [sem(f"x_ps_made{l}") for l in range(2)]
        x_sb_made = [sem(f"x_sb_made{l}") for l in range(2)]
        layer_out_made = sem("layer_out_made")
        z_half_made = sem("z_half_made")
        z_low_made = sem("z_low_made")
        z_made = sem("z_made")
        dense_loaded = sem("dense_loaded")
        mlp_loaded = sem("mlp_loaded")
        dense_turned = sem("dense_turned")
        dense_made = sem("dense_made")
        mlp_done = sem("mlp_done")
        hidden_made = sem("hidden_made")
        y_made = sem("y_made")
        y_written = sem("y_written")

        def out_count(layer, p):
            if layer == 0:
                return 1 if isinstance(p, int) and p == 0 else 3 * p
            if isinstance(p, int) and p == PAIRS - 1:
                return 3 * p + (2 if layer == 1 else 3)
            return 3 * p + (2 if layer == 1 else 4)

        def wait_layer(eng, layer, it, h):
            last = STEPS - 1
            steps, used = (pool_steps, pool_used) if last in pool_steps(it, h, layer) else (dve_steps, dve_used)
            eng.wait_ge(used, made_before(steps, it, h, layer) + len(steps(it, h, layer)))

        def wait_first_step(eng, p, it, h, block):
            if isinstance(p, int) and p < NEAR_FIRST:
                eng.wait_ge(near_loaded[p], 16)
            else:
                eng.wait_ge(x0_loaded[block_slot(h, block)], block_loads(it, h, block))

        def block_slot(h, block):
            return 2 * h + block if block < 2 else 2 + block

        def block_loads(it, h, block):
            return 16 * (it + 1) if block < 2 else 16 * (2 * it + h + 1)

        def staged(tile):
            return 16 * (KEPT // F_TILE) + 32 * tile

        def copied(tile):
            return 16 * (KEPT // F_TILE + tile)

        def rows_of(tile):
            return x0_rows[bass.ts(tile, KEPT), :]

        def turned(j):
            first = j % 2 * CHUNK + j // 2 * P
            return x0_rot_ps[:, first:first + P]

        def step_at(layer, t):
            return (FIRST_STEP[layer] + t) % STEPS

        def x0_step(h, layer, t, width=1):
            t = step_at(layer, t)
            return x0_wide[:, block_slot(h, t // BLOCK), (t % BLOCK) * WIDE:(t % BLOCK + width) * WIDE]

        def iterations(eng, body):
            body(0)
            with eng.Fori(1, TILES - 2) as it:
                body(it)
            body(TILES - 2)
            body(TILES - 1)

        def there(it, ahead):
            return not isinstance(it, int) or it + ahead < TILES

        block = ctx.enter_context(nc.Block())

        @block.sync
        def _(sp):
            def stage(tile, first, src):
                rows = rows_of(tile).rearrange("f (d b) -> (f d) b", b=P).rearrange("(j p) b -> p j b", p=P)
                n = src[1] - src[0]
                sp.dma_start(rows[:, first:first + n, :], x0_t[:, src[0]:src[1], :]).then_inc(x0_staged, 16)

            def copy_rows(tile, h, first, last):
                src = rows_of(tile)[first:last, h * WIDE:(h + 1) * WIDE].unsqueeze(1).broadcast_to([last - first, Q, WIDE])
                dst = x0_copies[bass.ts(2 * tile + h, COPIED * Q), :].rearrange("(f q) n -> f q n", q=Q)
                sp.dma_start(dst[first - FIRST_FIELD:last - FIRST_FIELD], src).then_inc(x0_copied[h], 16)

            def stage_tile(tile):
                stage(tile, 0, (0, ROW_TILES))
                stage(tile, ROW_TILES, (0, KEPT // F_TILE - ROW_TILES))

            def copy_tile(tile, h):
                if h == 0:
                    sp.wait_ge(x0_staged, staged(tile))
                    sp.nop(nofuse=True)
                copy_rows(tile, h, FIRST_FIELD, FIRST_FIELD + COPIED)

            def load_steps(dst, tile, h, first, apart, sem):
                rows = x0_copies[bass.ts(2 * tile + h, COPIED * Q), :][first * Q:]
                row = rows.ap[0][0]
                src = bass.AP(rows.tensor, rows.offset,
                              [[row, P], [apart * Q * row, dst.ap[1][1]], list(rows.ap[1])])
                sp.dma_start(dst, src).then_inc(sem, 16)

            def load_block(tile, h, blk):
                slot = block_slot(h, blk)
                load_steps(x0_wide[:, slot, :].rearrange("p (t n) -> p t n", n=WIDE), tile, h, blk * BLOCK, 1,
                           x0_loaded[slot])

            def load_rot(tile, h):
                for q in range(Q):
                    rows = rows_of(tile)[Q - 1 - q:Q - 1 - q + FIELDS, h * WIDE:(h + 1) * WIDE]
                    sp.dma_start(x0_rot[q:P:Q, :], rows).then_inc(rot_loaded, 16)

            def load_near(tile, h):
                load_steps(x0_wide[:, 2 * h:2 * h + 2, 0:WIDE], tile, h, 0, BLOCK, near_loaded[2 * tile + h])

            def load_after_near(tile, h):
                for blk in range(2):
                    slot = block_slot(h, blk)
                    load_steps(x0_wide[:, slot, WIDE:].rearrange("p (t n) -> p t n", n=WIDE), tile, h, blk * BLOCK + 1, 1,
                               x0_loaded[slot])

            def load_far(tile, h):
                load_steps(l0_tiles[:, 2:4, :], tile, h, 2 * BLOCK, BLOCK, far_loaded)

            def block_read(it, h, blk):
                last = (BLOCK * blk - FIRST_STEP[2]) % STEPS + BLOCK
                def through(steps):
                    return made_before(steps, it, h, 2) + sum(t < last for t in steps(it, h, 2))

                sp.wait_ge(dve_made, through(dve_steps))
                sp.nop(nofuse=True)
                if not isinstance(it, int) or through(pool_steps) > 0:
                    sp.wait_ge(pool_made, through(pool_steps))
                    sp.nop(nofuse=True)

            def load_operands(tile, h, p):
                sp.wait_ge(x0_copied[h], copied(tile))
                sp.nop(nofuse=True)
                sp.wait_ge(layer0_done, p + 2)
                sp.nop(nofuse=True)
                load_far(tile, h)
                load_rot(tile, h)

            sp.dma_start(idx[:], ids.rearrange("(t p) f -> p t f", p=P)).then_inc(idx_loaded, 16)
            sp.dma_start(dense, dense_ctx.rearrange("(t p) f -> p t f", p=P)).then_inc(dense_loaded, 16)
            sp.dma_start(ident_sb[:], ident).then_inc(weights, 16)
            sp.dma_start(w0_sb[:], w0_ab).then_inc(weights, 16)
            sp.dma_start(w0d_sb[:], w0_diag).then_inc(weights, 16)
            sp.dma_start(w_sb[0][:], w1).then_inc(weights, 16)
            sp.dma_start(w_sb[1][:], w2).then_inc(weights, 16)
            sp.dma_start(two_orders_sb, two_orders).then_inc(weights_b, 16)
            sp.dma_start(w0b_sb[:], w0_ba).then_inc(weights_b, 16)
            parts = 0
            for j in range(ROW_TILES):
                sp.wait_ge(x0_t_made, j + 1)
                fields = [(j * F_TILE, j)] + ([(FIELDS + j * F_TILE, ROW_TILES + j)] if j < KEPT // F_TILE - ROW_TILES
                                              else [])
                for field, place in fields:
                    stage(0, place, (j, j + 1))
                    parts += 1
                sp.wait_ge(x0_staged, 16 * parts)
                for h in range(2):
                    for field, place in fields:
                        copy_rows(0, h, max(field, FIRST_FIELD), min(field + F_TILE, FIRST_FIELD + COPIED))
            load_rot(0, 0)
            sp.wait_ge(x0_copied[0], copied(0))
            load_near(0, 0)
            load_far(0, 0)
            load_after_near(0, 0)
            load_block(0, 0, 2)
            load_block(0, 0, 3)
            sp.wait_ge(x0_copied[1], copied(0))
            load_near(0, 1)
            sp.wait_ge(layer0_done, 1)
            load_rot(0, 1)
            load_far(0, 1)
            sp.wait_ge(tile1_gathered, 16 * FIELDS)
            load_after_near(0, 1)
            sp.wait_ge(x0_t_made, ROW_TILES + 1)
            stage_tile(1)

            def body(it):
                for h in range(2):
                    p = 2 * it + h
                    start = isinstance(it, int) and it + h == 0
                    if there(it, 1) and not start:
                        load_operands(it + 1, h, p)
                    for blk in (2, 3):
                        if h == 0 or there(it, 1):
                            block_read(it, h, blk)
                            load_block(it + h, 1 - h, blk)
                        if start and blk == 2:
                            copy_tile(1, 0)
                        if blk == 2 and h == 1 and there(it, 2):
                            sp.wait_ge(x0_t_made, ROW_TILES + it + 2)
                            sp.nop(nofuse=True)
                            stage_tile(it + 2)
                    if start:
                        load_operands(1, 0, 0)
                    if start:
                        block_read(0, 0, 1)
                        load_near(1, 0)
                        load_after_near(1, 0)
                    elif there(it, 1):
                        for blk in (0, 1):
                            block_read(it, h, blk)
                            load_block(it + 1, h, blk)
                    if start:
                        copy_tile(1, 1)
                    if h == 1 and there(it, 2):
                        copy_tile(it + 2, 0)
                        copy_tile(it + 2, 1)

            iterations(sp, body)
            block_read(TILES - 1, 0, 1)
            sp.dma_start(wt1[:, 0, :], w_top1[0:P, :]).then_inc(mlp_loaded, 16)
            sp.dma_start(wt1[0:REST, 1, :], w_top1[P:, :]).then_inc(mlp_loaded, 16)
            sp.dma_start(wt2, w_top2.rearrange("(c p) j -> p c j", p=P)).then_inc(mlp_loaded, 16)
            sp.dma_start(wt3, w_top3).then_inc(mlp_loaded, 16)
            sp.dma_start(b1, b_top1).then_inc(mlp_loaded, 16)
            sp.dma_start(b2, b_top2).then_inc(mlp_loaded, 16)
            sp.wait_ge(y_made, BATCH // HALF)
            sp.dma_start(out.rearrange("n a -> a n"), y_sb).then_inc(y_written, 16)
            sp.wait_ge(y_written, 16)

        @block.gpsimd
        def _(pool):
            def gather(slot, fields, into=gathered):
                for f in fields:
                    pool.indirect_dma_start(
                        into[:, f * DIM:(f + 1) * DIM], None, tables[f],
                        bass.IndirectOffsetOnAxis(ap=idx[:, slot, f:f + 1], axis=0)).then_inc(
                            (first_gathered[f * DIM // P], tile1_gathered, rows_gathered)[slot], 16)

            def phase(it, h, layer):
                p = 2 * it + h
                first = isinstance(it, int) and it == 0
                shares = of_tile(it, GATHERED_FIRST, GATHERED, None)

                def gather_share(i):
                    if shares and shares[h, layer][i]:
                        field = sum(sum(shares[phase]) for phase in PHASES[:PHASES.index((h, layer))])
                        field += sum(shares[h, layer][:i])
                        if field == 0 and first:
                            pool.wait_ge(turned_made, ROW_TILES)
                        elif field == 0:
                            pool.wait_ge(rows_gathered, 16 * FIELDS * it)
                            nc.gpsimd.tensor_copy(idx[:, 2:3, :], idx[:, bass.ds(it + 2, 1), :]).then_inc(idx_moved, 1)
                            pool.wait_ge(idx_moved, it)
                            pool.wait_ge(turned_made, ROW_TILES * (it + 2))
                            pool.nop(nofuse=True)
                        gather(2, range(field, field + shares[h, layer][i]))

                gather_share(0)
                for i, t in enumerate(pool_steps(it, h, layer)):
                    n = made_before(pool_steps, it, h, layer) + i
                    if i == 0:
                        pool.wait_ge(x_sb_made[layer - 1], 4 * p + 4)
                    if first and i == 0:
                        pool.wait_ge(turned_made, 2 * ROW_TILES)
                    if layer == 1:
                        pool.wait_ge(x0_loaded[block_slot(h, t // BLOCK)], block_loads(it, h, t // BLOCK))
                    if not isinstance(n, int) or n >= POOL_RING:
                        pool.wait_ge(pool_used, n - POOL_RING + 1)
                    slot = ring_slot(pool_steps, POOL_RING, it, h, layer, i)
                    nc.gpsimd.tensor_tensor(pool_ring[:, slot, :], x0_step(h, layer, t), x_sb[layer - 1][:],
                                            ALU.mult).then_inc(pool_made, 1)
                    gather_share(i + 1)

            pool.wait_ge(idx_loaded, 16)
            gather(0, range(FIELDS))
            pool.wait_ge(w0_added, 2)
            gather(1, range(FIELDS), into=gathered1)

            def body(it):
                for h, layer in PHASES:
                    phase(it, h, layer)

            iterations(pool, body)

        @block.scalar
        def _(act):
            def take_turned(tile):
                act.wait_ge(turned_made, ROW_TILES * (tile + 1))
                act.wait_ge(x0_staged, staged(tile - 1))
                if isinstance(tile, int) and tile == 1:
                    nc.scalar.copy(x0_t[:].rearrange("p j b -> p (j b)"), acc[0][:]).then_inc(x0_t_made, 1)
                else:
                    rows = x0_rot_ps[:].rearrange("p (k s b) -> p s k b", k=2, b=P)[:, 0:ROW_TILES // 2]
                    nc.scalar.copy(x0_t[:].rearrange("p (s k) b -> p s k b", k=2), rows).then_inc(x0_t_made, 1)

            def take_x0(p, it, h, tile):
                act.wait_ge(x0_t_made, ROW_TILES + tile)
                act.wait_ge(rot_loaded, 16 * Q * (p + 1))
                if not isinstance(p, int) or p > 0:
                    act.wait_ge(l0_made, SHIFT_TILES * p)
                nc.scalar.copy(x0_rot_ps[:], x0_rot[:]).then_inc(rot_ps_made, 1)
                act.wait_ge(rot_ps_made, p + 1)
                wait_first_step(act, p, it, h, 0)
                nc.scalar.activation(x0_rot[:], x0_step(h, 1, 0), ACT.Square,
                                     scale=Q ** -0.5).then_inc(squares_made, 1)

            def finish(layer, p, h, tile):
                a = acc[h]
                if layer == 0:
                    act.wait_ge(layer0_done, p + 1)
                else:
                    wait_layer(act, layer, tile, h)
                if layer < 2:
                    for c in range(2):
                        for half in range(2):
                            nc.scalar.activation(x_ps[layer][half * HK:(half + 1) * HK, c * CHUNK:(c + 1) * CHUNK],
                                                 a[c * HK:(c + 1) * HK, :], ACT.Relu).then_inc(x_ps_made[layer], 1)
                if not isinstance(tile, int) or tile > 0:
                    act.wait_ge(z_half_made, LAYERS * (tile - 1) + (layer + 1))
                nc.scalar.activation(layer_out[:, layer, h, :], a[:], ACT.Relu).then_inc(layer_out_made, 1)
                if layer < 2:
                    act.wait_ge(layer_out_made, out_count(layer, p))
                    for c in range(2):
                        for half in range(2):
                            nc.scalar.copy(x_sb[layer][half * HK:(half + 1) * HK, c * CHUNK:(c + 1) * CHUNK],
                                           layer_out[c * HK:(c + 1) * HK, layer, h, :]).then_inc(x_sb_made[layer], 1)

            def lower(layer, tile):
                act.wait_ge(z_half_made, LAYERS * tile + (layer + 1))
                if not isinstance(tile, int) or tile + layer > 0:
                    act.wait_ge(z_made, LAYERS * tile + layer)
                nc.scalar.copy(z_low[:], z_half[HK:P, :]).then_inc(z_low_made, 1)

            def hidden(i):
                layer, n, j = MLP_ORDER[i]
                bias, dst = ((b1, h1), (b2, h2))[layer - 1]
                act.wait_ge(mlp_done, i + 1)
                nc.scalar.activation(dst[:, j, n * HALF:(n + 1) * HALF], mlp_banks[i % len(mlp_banks)], ACT.Relu,
                                     bias=bias[:, j:j + 1]).then_inc(hidden_made, 1)

            act.wait_ge(dense_turned, 1)
            for c in range(2):
                nc.scalar.copy(features[HK:REST, 1, c * CHUNK:(c + 1) * CHUNK],
                               x0_rot_ps[0:DIM, c * CHUNK:(c + 1) * CHUNK]).then_inc(dense_made, 1)
            for j in range(ROW_TILES):
                act.wait_ge(turned_made, j + 1)
                nc.scalar.copy(x0_t[:, j, :], turned(j)).then_inc(x0_t_made, 1)
            take_x0(0, 0, 0, 0)
            finish(0, 0, 0, 0)

            def body(it):
                for h in range(2):
                    p = 2 * it + h
                    if h == 0 or there(it, 1):
                        start = isinstance(it, int) and it + h == 0
                        take_x0(p + 1, it + h, 1 - h, it if start or not there(it, 1) else it + 1)
                    finish(1, p, h, it)
                    if h == 1:
                        lower(0, it)
                    elif not (isinstance(it, int) and it == 0):
                        lower(2, it - 1)
                    if h == 0 and isinstance(it, int) and it == 0:
                        take_turned(1)
                    if h == 0:
                        finish(0, p + 1, 1, it)
                    elif there(it, 1):
                        finish(0, p + 1, 0, it + 1)
                    if h == 1 and there(it, 2):
                        take_turned(it + 2)
                    if h == 1 and not there(it, 1):
                        for i in range(MLP_EARLY):
                            hidden(i)
                    if h == 1:
                        lower(1, it)
                    finish(2, p, h, it)

            iterations(act, body)
            lower(2, TILES - 1)
            for i in range(MLP_EARLY, len(MLP_ORDER)):
                hidden(i)
            done = len(MLP_ORDER)
            for n in range(BATCH // HALF):
                done += 1
                act.wait_ge(mlp_done, done)
                nc.scalar.copy(y_sb[:, n * HALF:(n + 1) * HALF], acc[n][32 * n:32 * n + 1, :]).then_inc(y_made, 1)

        @block.vector
        def _(dve):
            def products(it, h, layer, between):
                p = 2 * it + h
                i = 0
                block_of_last = -1
                between = dict(between)
                for group in dve_groups(it, h, layer):
                    t, width = group[0], len(group)
                    if i == 0:
                        dve.wait_ge(x_ps_made[layer - 1], 4 * p + 4)
                    if layer == 1 and t // BLOCK > block_of_last:
                        block_of_last = t // BLOCK
                        dve.wait_ge(x0_loaded[block_slot(h, block_of_last)], block_loads(it, h, block_of_last))
                    n = made_before(dve_steps, it, h, layer) + (i + width - 1)
                    if not isinstance(n, int) or n >= DVE_RING:
                        dve.wait_ge(dve_used, n - DVE_RING + 1)
                    slot = ring_slot(dve_steps, DVE_RING, it, h, layer, i)
                    nc.vector.tensor_tensor(
                        dve_ring[:, slot:slot + width, :],
                        x0_step(h, layer, t, width).rearrange("p (s n) -> p s n", n=WIDE),
                        x_ps[layer - 1][:].unsqueeze(1).broadcast_to([P, width, WIDE]),
                        ALU.mult).then_inc(dve_made, width)
                    i += width
                    for first in sorted(between):
                        if first <= i:
                            between.pop(first)()

            def sum_over_d(layer, tile):
                dve.wait_ge(layer_out_made, out_count(layer, 2 * tile + 1))
                if not isinstance(tile, int) or tile + layer > 0:
                    dve.wait_ge(z_low_made, LAYERS * tile + layer)
                    dve.wait_ge(z_made, LAYERS * tile + layer)
                nc.vector.tensor_reduce(z_half[:],
                                        layer_out[:, layer].rearrange("p h (d b) -> p b (h d)", b=P),
                                        AX_X, ALU.add).then_inc(z_half_made, 1)

            def join_chunks(layer, tile):
                rows = slice(HK, P) if layer == 1 else slice(0, HK)
                dve.wait_ge(z_low_made, LAYERS * tile + (layer + 1))
                nc.vector.tensor_tensor(features[rows, layer // 2, bass.ts(tile, P)], z_half[0:HK, :],
                                        z_low[:], ALU.add).then_inc(z_made, 1)

            def l0_products(p, it, h, tiles):
                for t in tiles:
                    operand = l0_tiles[:, t, :]
                    if t == 0:
                        dve.wait_ge(rot_ps_made, p + 1)
                    if t < 2:
                        operand = x0_step(h, 1, BLOCK * t)
                        wait_first_step(dve, p, it, h, t)
                    if t == 0 and (not isinstance(p, int) or p > 0):
                        dve.wait_ge(layer0_done, p)
                    if t == 2:
                        dve.wait_ge(far_loaded, 16 * (p + 1))
                    nc.vector.tensor_tensor(l0_tiles[:, t, :], operand, x0_rot_ps[:], ALU.mult).then_inc(l0_made, 1)

            dve.wait_ge(weights, 80)
            dve.wait_ge(weights_b, 32)
            nc.vector.tensor_tensor(w0b_sb, w0b_sb, two_orders_sb.unsqueeze(2).broadcast_to([P, SHIFT_TILES, HK]),
                                    ALU.mult).then_inc(w0_added, 1)
            dve.wait_ge(w0_added, 1)
            nc.vector.tensor_tensor(w0_sb[:], w0_sb[:], w0b_sb, ALU.add).then_inc(w0_added, 1)
            l0_products(0, 0, 0, l0_order(0))

            def body(it):
                first = isinstance(it, int) and it == 0
                for h in range(2):
                    p = 2 * it + h
                    ahead = h == 0 or there(it, 1)
                    products(it, h, 1, {len(dve_steps(it, h, 1)) - i: lambda part=tiles: l0_products(p + 1, it + h, 1 - h, l0_order(p + 1)[part])
                                        for i, tiles in L0_EARLY.items()} if ahead else {})
                    if h == 1:
                        sum_over_d(0, it)
                    elif not first:
                        sum_over_d(2, it - 1)
                    if ahead:
                        l0_products(p + 1, it + h, 1 - h, l0_order(p + 1)[L0_LATE])
                    if h == 1:
                        products(it, h, 2, {3: lambda: join_chunks(0, it), 6: lambda: sum_over_d(1, it),
                                            10: lambda: join_chunks(1, it)})
                    else:
                        products(it, h, 2, {} if first else {3: lambda: join_chunks(2, it - 1)})

            iterations(dve, body)
            sum_over_d(2, TILES - 1)
            join_chunks(2, TILES - 1)

        @block.tensor
        def _(pe):
            def turn(place, rows, j):
                nc.tensor.transpose(place, rows[:, j * P:(j + 1) * P], ident_sb[:]).then_inc(turned_made, 1)

            def turn_tile(tile, p):
                pe.wait_ge(rows_gathered, 16 * FIELDS * (tile - 1))
                pe.wait_ge(l0_made, SHIFT_TILES * (p + 2))
                for j in range(ROW_TILES):
                    turn(turned(j), gathered, j)

            def turn_tile1():
                pe.wait_ge(tile1_gathered, 16 * FIELDS)
                pe.wait_ge(layer_out_made, out_count(1, 0))
                for j in range(ROW_TILES):
                    turn(acc[0][:, j * P:(j + 1) * P], gathered1, j)

            def layer0(p, h):
                if not isinstance(p, int) or p > 1:
                    pe.wait_ge(layer_out_made, 3 * p - 2)
                for i, t in enumerate(l0_order(p)):
                    if i == SHIFT_TILES - 1 and isinstance(p, int) and p == 1:
                        turn_tile1()
                    pe.wait_ge(l0_made, SHIFT_TILES * p + i + 1)
                    for c in range(2):
                        nc.tensor.matmul(acc[h][c * HK:(c + 1) * HK, :], w0_sb[:, t, :],
                                                l0_tiles[:, t, c * CHUNK:(c + 1) * CHUNK], start=(i == 0), stop=False)
                pe.wait_ge(squares_made, p + 1)
                for c in range(2):
                    last = nc.tensor.matmul(acc[h][c * HK:(c + 1) * HK, :], w0d_sb[:],
                                            x0_rot[:, c * CHUNK:(c + 1) * CHUNK], start=False, stop=True)
                last.then_inc(layer0_done, 1)

            def contract(it, h, layer, between):
                p = 2 * it + h
                pe.wait_ge(layer_out_made, out_count(layer - 1, p))
                i_dve = i_pool = 0
                groups = dve_groups(it, h, layer)
                starts = {group[0]: len(group) for group in groups}
                ends = {group[-1]: len(group) for group in groups}
                for t in range(STEPS):
                    if t in pool_steps(it, h, layer):
                        pe.wait_ge(pool_made, made_before(pool_steps, it, h, layer) + i_pool + 1)
                        tile = pool_ring[:, ring_slot(pool_steps, POOL_RING, it, h, layer, i_pool), :]
                        used, n_used = pool_used, 1
                        i_pool += 1
                    else:
                        if t in starts:
                            pe.wait_ge(dve_made, made_before(dve_steps, it, h, layer) + (i_dve + starts[t]))
                        tile = dve_ring[:, ring_slot(dve_steps, DVE_RING, it, h, layer, i_dve), :]
                        used, n_used = dve_used, ends.get(t, 0)
                        i_dve += 1
                    for c in range(2):
                        last = nc.tensor.matmul(acc[h][c * HK:(c + 1) * HK, :], w_sb[layer - 1][:, step_at(layer, t), :],
                                                tile[:, c * CHUNK:(c + 1) * CHUNK],
                                                start=(t == 0), stop=(t == STEPS - 1))
                    if n_used:
                        last.then_inc(used, n_used)
                    if t in between:
                        between[t]()

            def mlp_product(i):
                layer, n, j = MLP_ORDER[i]
                cols, out_cols = slice(n * HALF, (n + 1) * HALF), slice(j * P, (j + 1) * P)
                bank = mlp_banks[i % len(mlp_banks)]
                if i == 0:
                    pe.wait_ge(mlp_loaded, MLP_LOADS)
                if layer == 1 and j == 0:
                    pe.wait_ge(z_made, LAYERS * HALF // P * (n + 1))
                if i >= len(mlp_banks):
                    pe.wait_ge(hidden_made, i - len(mlp_banks) + 1)
                if layer == 1:
                    nc.tensor.matmul(bank, wt1[:, 0, out_cols], features[:, 0, cols], start=True, stop=False)
                    last = nc.tensor.matmul(bank, wt1[0:REST, 1, out_cols], features[0:REST, 1, cols],
                                            start=False, stop=True)
                else:
                    for c in range(H1 // P):
                        if j == 0:
                            pe.wait_ge(hidden_made, i - H1 // P + c + 1)
                        last = nc.tensor.matmul(bank, wt2[:, c, out_cols], h1[:, c, cols],
                                                start=(c == 0), stop=(c == H1 // P - 1))
                last.then_inc(mlp_done, 1)

            pe.wait_ge(dense_loaded, 16)
            pe.wait_ge(weights, 80)
            for t in range(TILES):
                last = nc.tensor.matmul(x0_rot_ps[0:DIM, t * P:(t + 1) * P],
                                        dense[:, t, :], ident_sb[:], start=True, stop=True)
            last.then_inc(dense_turned, 1)
            pe.wait_ge(dense_made, 2)
            for j in range(ROW_TILES):
                pe.wait_ge(first_gathered[j], 16 * FIELDS // ROW_TILES)
                if j >= 2:
                    pe.wait_ge(x0_t_made, j - 1)
                turn(turned(j), gathered, j)
            for _ in range(WARM_UP):
                nc.tensor.matmul(acc[1][:, 0:P], ident_sb[:], ident_sb[:], start=True, stop=True)
            pe.wait_ge(w0_added, 2)
            layer0(0, 0)

            def body(it):
                for h in range(2):
                    p = 2 * it + h
                    ahead = h == 0 or there(it, 1)

                    contract(it, h, 1, {})
                    if ahead:
                        layer0(p + 1, 1 - h)
                    else:
                        for i in range(MLP_EARLY):
                            mlp_product(i)
                    if isinstance(it, int) and it + h == 0:
                        pe.wait_ge(x0_t_made, ROW_TILES + 1)
                    contract(it, h, 2, {3: lambda: turn_tile(it + 2, p)} if h == 1 and there(it, 2) else {})

            iterations(pe, body)

            for i in range(MLP_EARLY, len(MLP_ORDER)):
                mlp_product(i)
            for n in range(BATCH // HALF):
                for c in range(H2 // P):
                    pe.wait_ge(hidden_made, MLP_ORDER.index((2, n, c)) + 1)
                    last = nc.tensor.matmul(acc[n][32 * n:32 * n + 1, :], wt3[:, c:c + 1],
                                            h2[:, c, n * HALF:(n + 1) * HALF],
                                            start=(c == 0), stop=(c == H2 // P - 1))
                last.then_inc(mlp_done, 1)


def kernel(**inputs):
    import numpy as np
    import concourse.bacc as bacc
    from concourse.bass_utils import run_bass_kernel_spmd

    w0 = np.asarray(inputs["L0_rec_W0"])
    p, t = np.meshgrid(np.arange(P), np.arange(SHIFT_TILES), indexing="ij")
    m, q = p // Q, p % Q
    a = (m + Q - 1 - q) % FIELDS
    b = (m + BLOCK * t + FIRST_FIELD) % FIELDS
    square = (np.arange(P) // Q + FIRST_FIELD) % FIELDS
    arrays = {"w0_ab": w0[a, b], "w0_ba": w0[b, a], "w0_diag": w0[square, square],
              "two_orders": (BLOCK * t + 1 + q != FIELDS // 2).astype(np.float32),
              "ident": np.eye(P, dtype=np.float32)}
    for name in ("b_top1", "b_top2", "W_top3"):
        arrays[name] = np.asarray(inputs[name]).reshape(-1, P).T
    for name in ["dense_ctx", "ids", "W_top1", "W_top2"] + \
            [f"tbl_{f}" for f in range(FIELDS)]:
        arrays[name] = np.asarray(inputs[name])

    p, step = np.meshgrid(np.arange(P), np.arange(STEPS), indexing="ij")
    for layer in (1, 2):
        arrays[f"w{layer}"] = np.asarray(inputs[f"L0_rec_W{layer}"])[(p // Q + step + FIRST_FIELD) % FIELDS, p % HK]

    nc = bacc.Bacc("TRN2", target_bir_lowering=False, num_devices=1)
    ap, feed = {}, {}
    for name, value in arrays.items():
        feed[f"in_{name}"] = np.ascontiguousarray(value)
        ap[name] = nc.dram_tensor(f"in_{name}", value.shape, mybir.dt.from_np(value.dtype), kind="ExternalInput").ap()
    out = nc.dram_tensor("out_y", (BATCH, 1), F32, kind="ExternalOutput").ap()
    cin_tower(nc, ap["dense_ctx"], ap["ids"], [ap[f"tbl_{f}"] for f in range(FIELDS)], ap["W_top1"], ap["b_top1"],
              ap["W_top2"], ap["b_top2"], ap["W_top3"], ap["w0_ab"], ap["w0_ba"], ap["w0_diag"], ap["two_orders"],
              ap["w1"], ap["w2"], ap["ident"], out)
    result = run_bass_kernel_spmd(nc, [feed], core_ids=[0])
    return result.results[0]["out_y"]
```
